# Optimizing a Trainium2 kernel written in Bass

```python
import numpy as np
import jax
import jax.numpy as jnp

def _softmax(x, axis=-1):
    return jax.nn.softmax(x, axis=axis)

def _gelu(x):
    return jax.nn.gelu(x, approximate=True)

def _silu(x):
    return jax.nn.silu(x)

def _sigmoid(x):
    return jax.nn.sigmoid(x)

def _layernorm(x, axis=-1, eps=1e-05):
    m = jnp.mean(x, axis=axis, keepdims=True)
    v = jnp.var(x, axis=axis, keepdims=True)
    return (x - m) / jnp.sqrt(v + eps)

def _scatter_add(tgt, idx, src, axis=0):
    return tgt.at[idx].add(src)

def _segment_sum(src, seg, n):
    return jax.ops.segment_sum(src, seg, n)
kernel_name = 'mk_sandwich_d1_jaxref_r8_9686e9'

def setup_inputs(seed: int=0):
    np.random.seed(seed)
    _w = jnp.asarray

    def _L0_attn_setup():
        import jax, jax.numpy as jnp
        import numpy as np
        from jax import lax
        D_MODEL = 128
        D_INNER = 256
        D_STATE = 16
        DT_RANK = 128
        K = 4
        EPS = 1e-05

        def _layer_norm(x, w, b):
            mu = jnp.mean(x, axis=-1, keepdims=True)
            var = jnp.mean(jnp.square(x - mu), axis=-1, keepdims=True)
            return (x - mu) * lax.rsqrt(var + EPS) * w + b

        def _causal_depthwise_conv(x, w, b):
            L = x.shape[1]
            xp = jnp.pad(x, ((0, 0), (K - 1, 0), (0, 0)))
            out = b
            for k in range(K):
                out = out + w[:, k] * xp[:, k:k + L, :]
            return out

        def _selective_scan(u, delta, A, B, C, D):
            deltaA = jnp.exp(jnp.einsum('bld,dn->bldn', delta, A))
            deltaBu = jnp.einsum('bld,bln,bld->bldn', delta, B, u)
            bsz, _, d, n = deltaA.shape

            def step(h, inp):
                dA, dBu, Ct = inp
                h = dA * h + dBu
                y = jnp.einsum('bdn,bn->bd', h, Ct)
                return (h, y)
            h0 = jnp.zeros((bsz, d, n), u.dtype)
            _, ys = lax.scan(step, h0, (deltaA.transpose(1, 0, 2, 3), deltaBu.transpose(1, 0, 2, 3), C.transpose(1, 0, 2)))
            y = ys.transpose(1, 0, 2)
            return y + u * D
        key = jax.random.key(seed)
        ks = jax.random.split(key, 12)
        x = jax.random.normal(ks[0], (2, 128, D_MODEL), dtype=jnp.float32)
        norm_w = jnp.ones((D_MODEL,), jnp.float32)
        norm_b = jnp.zeros((D_MODEL,), jnp.float32)
        in_proj_w = jax.random.normal(ks[1], (D_MODEL, 2 * D_INNER), jnp.float32) * D_MODEL ** (-0.5)
        conv_w = jax.random.normal(ks[2], (D_INNER, K), jnp.float32) * K ** (-0.5)
        conv_b = jnp.zeros((D_INNER,), jnp.float32)
        x_proj_w = jax.random.normal(ks[3], (D_INNER, DT_RANK + 2 * D_STATE), jnp.float32) * D_INNER ** (-0.5)
        dt_init_std = DT_RANK ** (-0.5)
        dt_proj_w = jax.random.uniform(ks[4], (DT_RANK, D_INNER), jnp.float32, -dt_init_std, dt_init_std)
        dt = jnp.exp(jax.random.uniform(ks[5], (D_INNER,), jnp.float32) * (np.log(0.1) - np.log(0.001)) + np.log(0.001))
        dt_proj_b = dt + jnp.log(-jnp.expm1(-dt))
        A_log = jax.random.normal(ks[6], (D_INNER, D_STATE), jnp.float32)
        D_param = jax.random.normal(ks[7], (D_INNER,), jnp.float32)
        out_proj_w = jax.random.normal(ks[8], (D_INNER, D_MODEL), jnp.float32) * D_INNER ** (-0.5)
        return dict(x=x, norm_w=norm_w, norm_b=norm_b, in_proj_w=in_proj_w, conv_w=conv_w, conv_b=conv_b, x_proj_w=x_proj_w, dt_proj_w=dt_proj_w, dt_proj_b=dt_proj_b, A_log=A_log, D_param=D_param, out_proj_w=out_proj_w)
    _L0_attn_in = _L0_attn_setup()

    def _L0_ffn_setup():
        import jax, jax.numpy as jnp
        import numpy as np
        E, H, I, TOP_K = (16, 128, 256, 4)
        ALPHA, LIMIT = (1.702, 7.0)
        BLK = 32
        FP4_LUT = jnp.array([0.0, 0.5, 1.0, 1.5, 2.0, 3.0, 4.0, 6.0, -0.0, -0.5, -1.0, -1.5, -2.0, -3.0, -4.0, -6.0], dtype=jnp.float32)

        def dequant_mxfp4(blocks, scales, in_dim):
            e, o, _ = blocks.shape
            lo = (blocks & 15).astype(jnp.int32)
            hi = (blocks >> 4).astype(jnp.int32)
            codes = jnp.stack([lo, hi], axis=-1).reshape(e, o, in_dim)
            vals = FP4_LUT[codes]
            scale = jnp.exp2(scales.astype(jnp.float32) - 127.0)
            w = vals.reshape(e, o, in_dim // BLK, BLK) * scale[..., None]
            return w.reshape(e, o, in_dim)

        def moe_forward(hidden_states, router_weight, router_bias, gate_proj_bias, up_proj_bias, down_proj_bias, gate_proj_blocks, gate_proj_scales, up_proj_blocks, up_proj_scales, down_proj_blocks, down_proj_scales):
            b, s, h = hidden_states.shape
            x = hidden_states.reshape(-1, h)
            t = x.shape[0]
            logits = x @ router_weight.T + router_bias
            top_v, top_i = jax.lax.top_k(logits, TOP_K)
            probs = jax.nn.softmax(top_v, axis=-1)
            routing = jnp.zeros((t, E), dtype=x.dtype).at[jnp.arange(t)[:, None], top_i].set(probs)
            wg = dequant_mxfp4(gate_proj_blocks, gate_proj_scales, h)
            wu = dequant_mxfp4(up_proj_blocks, up_proj_scales, h)
            wd = dequant_mxfp4(down_proj_blocks, down_proj_scales, I)
            gate = jnp.einsum('th,eih->eti', x, wg) + gate_proj_bias[:, None, :]
            up = jnp.einsum('th,eih->eti', x, wu) + up_proj_bias[:, None, :]
            gate = jnp.minimum(gate, LIMIT)
            up = jnp.clip(up, -LIMIT, LIMIT)
            glu = gate * jax.nn.sigmoid(gate * ALPHA)
            inter = (up + 1.0) * glu
            out_e = jnp.einsum('eti,ehi->eth', inter, wd) + down_proj_bias[:, None, :]
            out = jnp.einsum('eth,te->th', out_e, routing)
            return out.reshape(b, s, h)
        key = jax.random.key(seed)
        ks = jax.random.split(key, 10)
        inp = {'hidden_states': jax.random.normal(ks[0], (1, 128, H), dtype=jnp.float32), 'router_weight': jax.random.normal(ks[1], (E, H), dtype=jnp.float32) * 0.02, 'router_bias': jax.random.normal(ks[2], (E,), dtype=jnp.float32) * 0.02, 'gate_proj_bias': jax.random.normal(ks[3], (E, I), dtype=jnp.float32) * 0.02, 'up_proj_bias': jax.random.normal(ks[4], (E, I), dtype=jnp.float32) * 0.02, 'down_proj_bias': jax.random.normal(ks[5], (E, H), dtype=jnp.float32) * 0.02, 'gate_proj_blocks': jax.random.randint(ks[6], (E, I, H // 2), 0, 32, dtype=jnp.int32).astype(jnp.uint8), 'up_proj_blocks': jax.random.randint(ks[7], (E, I, H // 2), 0, 32, dtype=jnp.int32).astype(jnp.uint8), 'down_proj_blocks': jax.random.randint(ks[8], (E, H, I // 2), 0, 32, dtype=jnp.int32).astype(jnp.uint8), 'gate_proj_scales': jax.random.randint(jax.random.fold_in(key, 20), (E, I, H // BLK), 120, 128, dtype=jnp.int32).astype(jnp.uint8), 'up_proj_scales': jax.random.randint(jax.random.fold_in(key, 21), (E, I, H // BLK), 120, 128, dtype=jnp.int32).astype(jnp.uint8), 'down_proj_scales': jax.random.randint(jax.random.fold_in(key, 22), (E, H, I // BLK), 120, 128, dtype=jnp.int32).astype(jnp.uint8)}
        return inp
    _L0_ffn_in = _L0_ffn_setup()
    _d = {'L0_attn_x': _L0_attn_in['x'], 'L0_attn_norm_w': _L0_attn_in['norm_w'], 'L0_attn_norm_b': _L0_attn_in['norm_b'], 'L0_attn_in_proj_w': _L0_attn_in['in_proj_w'], 'L0_attn_conv_w': _L0_attn_in['conv_w'], 'L0_attn_conv_b': _L0_attn_in['conv_b'], 'L0_attn_x_proj_w': _L0_attn_in['x_proj_w'], 'L0_attn_dt_proj_w': _L0_attn_in['dt_proj_w'], 'L0_attn_dt_proj_b': _L0_attn_in['dt_proj_b'], 'L0_attn_A_log': _L0_attn_in['A_log'], 'L0_attn_D_param': _L0_attn_in['D_param'], 'L0_attn_out_proj_w': _L0_attn_in['out_proj_w'], 'L0_ffn_router_weight': _L0_ffn_in['router_weight'], 'L0_ffn_router_bias': _L0_ffn_in['router_bias'], 'L0_ffn_gate_proj_bias': _L0_ffn_in['gate_proj_bias'], 'L0_ffn_up_proj_bias': _L0_ffn_in['up_proj_bias'], 'L0_ffn_down_proj_bias': _L0_ffn_in['down_proj_bias'], 'L0_ffn_gate_proj_blocks': _L0_ffn_in['gate_proj_blocks'], 'L0_ffn_gate_proj_scales': _L0_ffn_in['gate_proj_scales'], 'L0_ffn_up_proj_blocks': _L0_ffn_in['up_proj_blocks'], 'L0_ffn_up_proj_scales': _L0_ffn_in['up_proj_scales'], 'L0_ffn_down_proj_blocks': _L0_ffn_in['down_proj_blocks'], 'L0_ffn_down_proj_scales': _L0_ffn_in['down_proj_scales']}
    _x0 = _d['L0_attn_x']
    _d['L0_attn_x'] = jax.random.normal(jax.random.fold_in(jax.random.key(seed), 1), (16, 512, 128), dtype=_x0.dtype)
    del _x0
    return _d

def reference(L0_attn_x, L0_attn_norm_w, L0_attn_norm_b, L0_attn_in_proj_w, L0_attn_conv_w, L0_attn_conv_b, L0_attn_x_proj_w, L0_attn_dt_proj_w, L0_attn_dt_proj_b, L0_attn_A_log, L0_attn_D_param, L0_attn_out_proj_w, L0_ffn_router_weight, L0_ffn_router_bias, L0_ffn_gate_proj_bias, L0_ffn_up_proj_bias, L0_ffn_down_proj_bias, L0_ffn_gate_proj_blocks, L0_ffn_gate_proj_scales, L0_ffn_up_proj_blocks, L0_ffn_up_proj_scales, L0_ffn_down_proj_blocks, L0_ffn_down_proj_scales):

    def _L0_attn_ref(x, norm_w, norm_b, in_proj_w, conv_w, conv_b, x_proj_w, dt_proj_w, dt_proj_b, A_log, D_param, out_proj_w):
        import jax, jax.numpy as jnp
        import numpy as np
        from jax import lax
        D_MODEL = 128
        D_INNER = 256
        D_STATE = 16
        DT_RANK = 128
        K = 4
        EPS = 1e-05

        def _layer_norm(x, w, b):
            mu = jnp.mean(x, axis=-1, keepdims=True)
            var = jnp.mean(jnp.square(x - mu), axis=-1, keepdims=True)
            return (x - mu) * lax.rsqrt(var + EPS) * w + b

        def _causal_depthwise_conv(x, w, b):
            L = x.shape[1]
            xp = jnp.pad(x, ((0, 0), (K - 1, 0), (0, 0)))
            out = b
            for k in range(K):
                out = out + w[:, k] * xp[:, k:k + L, :]
            return out

        def _selective_scan(u, delta, A, B, C, D):
            deltaA = jnp.exp(jnp.einsum('bld,dn->bldn', delta, A))
            deltaBu = jnp.einsum('bld,bln,bld->bldn', delta, B, u)
            bsz, _, d, n = deltaA.shape

            def step(h, inp):
                dA, dBu, Ct = inp
                h = dA * h + dBu
                y = jnp.einsum('bdn,bn->bd', h, Ct)
                return (h, y)
            h0 = jnp.zeros((bsz, d, n), u.dtype)
            _, ys = lax.scan(step, h0, (deltaA.transpose(1, 0, 2, 3), deltaBu.transpose(1, 0, 2, 3), C.transpose(1, 0, 2)))
            y = ys.transpose(1, 0, 2)
            return y + u * D
        residual = x
        h = _layer_norm(x, norm_w, norm_b)
        xr = h @ in_proj_w
        xs, res = (xr[..., :D_INNER], xr[..., D_INNER:])
        xs = _causal_depthwise_conv(xs, conv_w, conv_b)
        xs = jax.nn.silu(xs)
        A = -jnp.exp(A_log)
        xp = xs @ x_proj_w
        dr = xp[..., :DT_RANK]
        Bm = xp[..., DT_RANK:DT_RANK + D_STATE]
        Cm = xp[..., DT_RANK + D_STATE:]
        delta = jax.nn.softplus(dr @ dt_proj_w + dt_proj_b)
        y = _selective_scan(xs, delta, A, Bm, Cm, D_param)
        y = y * jax.nn.silu(res)
        return y @ out_proj_w + residual

    def _L0_ffn_ref(hidden_states, router_weight, router_bias, gate_proj_bias, up_proj_bias, down_proj_bias, gate_proj_blocks, gate_proj_scales, up_proj_blocks, up_proj_scales, down_proj_blocks, down_proj_scales):
        import jax, jax.numpy as jnp
        import numpy as np
        E, H, I, TOP_K = (16, 128, 256, 4)
        ALPHA, LIMIT = (1.702, 7.0)
        BLK = 32
        FP4_LUT = jnp.array([0.0, 0.5, 1.0, 1.5, 2.0, 3.0, 4.0, 6.0, -0.0, -0.5, -1.0, -1.5, -2.0, -3.0, -4.0, -6.0], dtype=jnp.float32)

        def dequant_mxfp4(blocks, scales, in_dim):
            e, o, _ = blocks.shape
            lo = (blocks & 15).astype(jnp.int32)
            hi = (blocks >> 4).astype(jnp.int32)
            codes = jnp.stack([lo, hi], axis=-1).reshape(e, o, in_dim)
            vals = FP4_LUT[codes]
            scale = jnp.exp2(scales.astype(jnp.float32) - 127.0)
            w = vals.reshape(e, o, in_dim // BLK, BLK) * scale[..., None]
            return w.reshape(e, o, in_dim)

        def moe_forward(hidden_states, router_weight, router_bias, gate_proj_bias, up_proj_bias, down_proj_bias, gate_proj_blocks, gate_proj_scales, up_proj_blocks, up_proj_scales, down_proj_blocks, down_proj_scales):
            b, s, h = hidden_states.shape
            x = hidden_states.reshape(-1, h)
            t = x.shape[0]
            logits = x @ router_weight.T + router_bias
            top_v, top_i = jax.lax.top_k(logits, TOP_K)
            probs = jax.nn.softmax(top_v, axis=-1)
            routing = jnp.zeros((t, E), dtype=x.dtype).at[jnp.arange(t)[:, None], top_i].set(probs)
            wg = dequant_mxfp4(gate_proj_blocks, gate_proj_scales, h)
            wu = dequant_mxfp4(up_proj_blocks, up_proj_scales, h)
            wd = dequant_mxfp4(down_proj_blocks, down_proj_scales, I)
            gate = jnp.einsum('th,eih->eti', x, wg) + gate_proj_bias[:, None, :]
            up = jnp.einsum('th,eih->eti', x, wu) + up_proj_bias[:, None, :]
            gate = jnp.minimum(gate, LIMIT)
            up = jnp.clip(up, -LIMIT, LIMIT)
            glu = gate * jax.nn.sigmoid(gate * ALPHA)
            inter = (up + 1.0) * glu
            out_e = jnp.einsum('eti,ehi->eth', inter, wd) + down_proj_bias[:, None, :]
            out = jnp.einsum('eth,te->th', out_e, routing)
            return out.reshape(b, s, h)
        return moe_forward(hidden_states, router_weight, router_bias, gate_proj_bias, up_proj_bias, down_proj_bias, gate_proj_blocks, gate_proj_scales, up_proj_blocks, up_proj_scales, down_proj_blocks, down_proj_scales)
    x = L0_attn_x
    x = x + _layernorm(_L0_attn_ref(_layernorm(x, axis=-1), L0_attn_norm_w, L0_attn_norm_b, L0_attn_in_proj_w, L0_attn_conv_w, L0_attn_conv_b, L0_attn_x_proj_w, L0_attn_dt_proj_w, L0_attn_dt_proj_b, L0_attn_A_log, L0_attn_D_param, L0_attn_out_proj_w), axis=-1)
    x = x + _layernorm(_L0_ffn_ref(_layernorm(x, axis=-1), L0_ffn_router_weight, L0_ffn_router_bias, L0_ffn_gate_proj_bias, L0_ffn_up_proj_bias, L0_ffn_down_proj_bias, L0_ffn_gate_proj_blocks, L0_ffn_gate_proj_scales, L0_ffn_up_proj_blocks, L0_ffn_up_proj_scales, L0_ffn_down_proj_blocks, L0_ffn_down_proj_scales), axis=-1)
    return x

_drawn_inputs = setup_inputs


def setup_inputs(seed=0):
    import zlib

    import numpy as np

    out = dict(_drawn_inputs(seed))
    spreads = {'L0_attn_norm_w': (1.0, 0.2), 'L0_attn_norm_b': (0.0, 0.1), 'L0_attn_conv_b': (0.0, 0.1)}
    factors = {'L0_ffn_gate_proj_bias': 37.09,
     'L0_ffn_up_proj_bias': 36.474,
     'L0_ffn_down_proj_bias': 64.0}
    for name, (base, spread) in spreads.items():
        noise = np.random.default_rng([zlib.crc32(name.encode()), seed]).standard_normal(out[name].shape)
        drawn = base * np.exp(spread * noise) if base else spread * noise
        out[name] = jnp.asarray(drawn.astype(out[name].dtype))
    for name, factor in factors.items():
        out[name] = (out[name] * factor).astype(out[name].dtype)
    return out
```

```python
from contextlib import ExitStack

import concourse.bass as bass
from concourse import mybir

F32, BF16, I32, U32, U8 = (mybir.dt.float32, mybir.dt.bfloat16, mybir.dt.int32,
                           mybir.dt.uint32, mybir.dt.uint8)
ALU = mybir.AluOpType
ACT = mybir.ActivationFunctionType
AX = mybir.AxisListType

P = 128
NB, L, DM = 16, 512, 128
DI, NS, TAPS = 256, 16, 4
HALF = DI // P
JT = L // P
TOKENS = NB * L
NE, FI, TOPK = 16, 256, 4
FH = FI // P
EPS = 1e-5
GATE_MAX, SIG_SCALE = 7.0, 1.702
TILE = 256
REGION = TOKENS + TILE
NT = TOKENS * TOPK // TILE + NE
ROW = 3 * DM + 2
NO_TOKEN = 1 << 20
CHUNKS, CW = 12, 1024
LN_EPS_N = JT


def build(nc, x, norm_w, norm_b, in_w, conv_w, conv_b, xp_w, dt_w, dt_b, a_log, d_par, out_w,
          rt_w, rt_b, g_bias, u_bias, d_bias, g_blk, g_scl, u_blk, u_scl, d_blk, d_scl, out):
    rows_d = nc.dram_tensor("expert_rows", ((NE + 1) * REGION, ROW // 2), U32).ap()
    yk_d = nc.dram_tensor("expert_out", (TOKENS * TOPK, DM), F32).ap()
    x1_d = nc.dram_tensor("x_mid", (NB, L, DM), F32).ap()
    with ExitStack() as ctx:
        def sb(name, shape, dt=F32):
            return ctx.enter_context(nc.sbuf_tensor(name, shape, dt))
        keep = dict(
            ident=sb("ident", [P, P]), identb=sb("identb", [P, P], BF16),
            w_all=sb("w_all", [P, CHUNKS * CW], BF16),
            wd32=sb("wd32", [P, NE * FH * DM]),
            bg=sb("bg", [P, NE * FH]), bu=sb("bu", [P, NE * FH]), bd=sb("bd", [1, NE * DM]),
            ones_row=sb("ones_row", [1, P]),
            base=sb("base", [P, NE]), ebase=sb("ebase", [P, NE]), iota_e=sb("iota_e", [P, NE]),
            prob=sb("prob", [P, NB * JT * TOPK]),
        )
        setup_phase(nc, keep, g_blk, g_scl, u_blk, u_scl, d_blk, d_scl, g_bias, u_bias, d_bias)
        mamba_phase(nc, keep, x, norm_w, norm_b, in_w, conv_w, conv_b, xp_w, dt_w, dt_b, a_log,
                    d_par, out_w, rt_w, rt_b, rows_d, x1_d)
        expert_phase(nc, keep, rows_d, yk_d)
        combine_phase(nc, keep, yk_d, x1_d, out)


def setup_phase(nc, keep, g_blk, g_scl, u_blk, u_scl, d_blk, d_scl, g_bias, u_bias, d_bias):
    ident, identb, w_all = keep["ident"], keep["identb"], keep["w_all"]
    with ExitStack() as ctx:
        def sb(name, shape, dt=F32):
            return ctx.enter_context(nc.sbuf_tensor(name, shape, dt))

        def sem(name):
            return ctx.enter_context(nc.semaphore(name))

        CB = CW // 2
        codes = sb("codes", [P, CHUNKS * CB], U8)
        scl8 = sb("scl8", [P, CHUNKS * 32], U8)
        codes_w, scl_w = codes[:].bitcast(U32), scl8[:].bitcast(U32)
        scl32 = sb("scl32", [P, CHUNKS * 32], I32)
        nib = sb("nib", [P, CW], U8)
        mag = sb("mag", [P, CW], U8)
        sgn = sb("sgn", [P, CW], U8)
        over4 = sb("over4", [P, CW], BF16)
        over6 = sb("over6", [P, CW], BF16)
        sfac = sb("sfac", [P, CW], BF16)
        val = sb("val", [P, CW], BF16)
        wq = sb("wq", [P, 2, CW], BF16)
        wps = [ctx.enter_context(nc.psum_tensor(f"wps{i}", [P, CW], BF16)) for i in range(2)]
        loaded, made, link, quant, turned, stored, passed = (sem(n) for n in (
            "loaded", "made", "link", "quant", "turned", "stored", "s_passed"))
        block = ctx.enter_context(nc.Block())

        @block.sync
        def _(sp):
            EC = NE // 4
            for m, (blk, scl) in enumerate(((g_blk, g_scl), (u_blk, u_scl))):
                for h in range(FH):
                    dst = codes_w[:, m * CB:(m + 1) * CB].rearrange(
                        "p (e h c) -> p e h c", e=NE, h=FH)[:, :, h, :]
                    sp.dma_start(dst, blk[:, h * P:(h + 1) * P, :].rearrange("e p c -> p e c")
                                 ).then_inc(loaded, 16)
                    dst = scl_w[:, m * 32:(m + 1) * 32].rearrange(
                        "p (e h c) -> p e h c", e=NE, h=FH)[:, :, h, :]
                    sp.dma_start(dst, scl[:, h * P:(h + 1) * P, :].rearrange("e p c -> p e c"),
                                 allow_slow_non_contiguous=True).then_inc(loaded, 16)
            sp.dma_start(codes_w[:, 2 * CB:].rearrange("p (e c) -> p e c", e=NE),
                         d_blk.rearrange("e p c -> p e c")).then_inc(loaded, 16)
            sp.dma_start(scl_w[:, 64:].rearrange("p (e c) -> p e c", e=NE),
                         d_scl.rearrange("e p c -> p e c")).then_inc(loaded, 16)
            for dst, src in ((keep["bg"], g_bias), (keep["bu"], u_bias)):
                for h in range(FH):
                    sp.dma_start(dst[:].rearrange("p (e h) -> p e h", h=FH)[:, :, h:h + 1],
                                 src[:, h * P:(h + 1) * P].rearrange("e (p o) -> p e o", o=1),
                                 allow_slow_non_contiguous=True).then_inc(loaded, 16)
            sp.dma_start(keep["bd"][:], d_bias.rearrange("(o e) h -> o (e h)", o=1)
                         ).then_inc(loaded, 16)
            sp.wait_ge(loaded, 15 * 16)

        @block.gpsimd
        def _(pool):
            nc.gpsimd.memset(ident[:], 0.0).then_inc(made, 1)
            pool.wait_ge(made, 1)
            nc.gpsimd.affine_select(out=ident[:], in_=ident[:], compare_op=ALU.not_equal,
                                    fill=1.0, base=0, pattern=[[-1, P]],
                                    channel_multiplier=1).then_inc(made, 1)
            pool.wait_ge(made, 2)
            nc.gpsimd.tensor_copy(identb[:], ident[:]).then_inc(made, 1)
            nc.gpsimd.iota(keep["iota_e"][:], [[1, NE]], base=0, channel_multiplier=0,
                           allow_small_or_imprecise_dtypes=True).then_inc(made, 1)
            pool.wait_ge(made, 4)
            nc.gpsimd.tensor_scalar(keep["ebase"][:], keep["iota_e"][:], float(REGION), None,
                                    ALU.mult).then_inc(made, 1)
            nc.gpsimd.memset(keep["ones_row"][:], 1.0).then_inc(made, 1)
            pool.wait_ge(made, 5)
            nc.gpsimd.tensor_copy(keep["base"][:], keep["ebase"][:]).then_inc(made, 1)

        STEPS = 11

        @block.vector
        def _(dve):
            dve.wait_ge(loaded, 15 * 16)
            nc.vector.tensor_copy(scl32[:], scl8[:]).then_inc(link, 1)
            dve.wait_ge(link, 1)
            nc.vector.tensor_scalar(scl32[:], scl32[:], 23, None,
                                    ALU.logical_shift_left).then_inc(link, 1)
            nc.vector.tensor_scalar(keep["bu"][:], keep["bu"][:], 1.0, None, ALU.add
                                    ).then_inc(link, 1)
            pair = nib[:].rearrange("p (c t) -> p c t", t=2)
            with dve.Fori(0, CHUNKS // 2) as i:
                for u in range(2):
                    c = i * 2 + u
                    at = c * STEPS + 3
                    src = codes[:, bass.ds(c * CB, CB)].rearrange("p (c o) -> p c o", o=1)
                    dve.wait_ge(link, at)
                    nc.vector.tensor_scalar(pair[:, :, 0:1], src, 15, None, ALU.bitwise_and
                                            ).then_inc(link, 1)
                    nc.vector.tensor_scalar(pair[:, :, 1:2], src, 4, None,
                                            ALU.logical_shift_right).then_inc(link, 1)
                    dve.wait_ge(link, at + 2)
                    nc.vector.tensor_scalar(mag[:], nib[:], 7, None, ALU.bitwise_and
                                            ).then_inc(link, 1)
                    nc.vector.tensor_scalar(sgn[:], nib[:], 8, None, ALU.bitwise_and
                                            ).then_inc(link, 1)
                    dve.wait_ge(link, at + 4)
                    nc.vector.tensor_scalar(over4[:], mag[:], -4.0, 0.0, ALU.add, ALU.max
                                            ).then_inc(link, 1)
                    nc.vector.tensor_scalar(over6[:], mag[:], -6.0, 0.0, ALU.add, ALU.max
                                            ).then_inc(link, 1)
                    nc.vector.tensor_scalar(sfac[:], sgn[:], -0.125, 0.5, ALU.mult, ALU.add
                                            ).then_inc(link, 1)
                    dve.wait_ge(link, at + 7)
                    nc.vector.tensor_tensor(val[:], mag[:], over4[:], ALU.add).then_inc(link, 1)
                    dve.wait_ge(link, at + 8)
                    nc.vector.scalar_tensor_tensor(val[:], over6[:], 2.0, val[:], ALU.mult,
                                                   ALU.add).then_inc(link, 1)
                    dve.wait_ge(link, at + 9)
                    nc.vector.tensor_tensor(val[:], val[:], sfac[:], ALU.mult).then_inc(link, 1)
                    dve.wait_ge(turned, c + 1)
                    dve.wait_ge(link, at + 10)
                    nc.vector.tensor_tensor(
                        wq[:, u, :].rearrange("p (b k) -> p b k", k=32),
                        val[:].rearrange("p (b k) -> p b k", k=32),
                        scl32[:, bass.ds(c * 32, 32)].bitcast(F32).rearrange(
                            "p (b o) -> p b o", o=1).to_broadcast([P, 32, 32]),
                        ALU.mult).then_inc(quant, 1)
                    dve.wait_ge(quant, c + 1)
                    nc.vector.sem_inc(link, 1)

        @block.tensor
        def _(pe):
            pe.sem_inc(turned, 2)
            pe.wait_ge(made, 3)
            with pe.Fori(0, CHUNKS // 2) as i:
                for u in range(2):
                    c = i * 2 + u
                    pe.wait_ge(quant, c + 1)
                    pe.wait_ge(stored, c + 1)
                    for t in range(CW // P):
                        last = nc.tensor.transpose(wps[u][:, t * P:(t + 1) * P],
                                                   wq[:, u, t * P:(t + 1) * P], identb[:])
                    last.then_inc(turned, 1)

        @block.scalar
        def _(act):
            act.sem_inc(stored, 2)
            with act.Fori(0, CHUNKS // 2) as i:
                for u in range(2):
                    c = i * 2 + u
                    act.wait_ge(turned, c + 3)
                    act.sem_inc(passed, 1)
                    nc.scalar.activation(w_all[:, bass.ds(c * CW, CW)], wps[u][:], ACT.Copy
                                         ).then_inc(stored, 1)
            act.wait_ge(stored, CHUNKS + 2)
            nc.scalar.activation(keep["wd32"][:], w_all[:, 8 * CW:], ACT.Copy)


def layernorm_stats(nc, src, st, mv):
    stats = [lambda j=j: nc.vector.bn_stats(st[:, j, :], src[:, j, :]) for j in range(JT)]
    aggr = [lambda j=j: nc.vector.bn_aggr(mv[:, j, :], st[:, j, :]) for j in range(JT)]
    return stats, aggr


def mamba_phase(nc, keep, x, norm_w, norm_b, in_w, conv_w, conv_b, xp_w, dt_w, dt_b, a_log,
                d_par, out_w, rt_w, rt_b, rows_d, x1_d):
    ident, identb = keep["ident"], keep["identb"]
    base, iota_e = keep["base"], keep["iota_e"]
    with ExitStack() as ctx:
        def sb(name, shape, dt=F32):
            return ctx.enter_context(nc.sbuf_tensor(name, shape, dt))

        def bank(name):
            return ctx.enter_context(nc.psum_tensor(name, [P, 512], F32))

        def sem(name):
            return ctx.enter_context(nc.semaphore(name))

        wx = sb("wx", [P, 2 * DI])
        cw = sb("cw", [P, DI, TAPS])
        wc = sb("wc", [P, TAPS, DI])
        xpw = sb("xpw", [P, HALF, P + 2 * NS])
        xpw3 = sb("xpw3", [P, HALF, 3, 2 * NS])
        dtw = sb("dtw", [P, DI])
        ow = sb("ow", [P, HALF, DM])
        a_neg = sb("a_neg", [P, HALF, NS])
        nw, nbias = sb("nw", [P, 1]), sb("nbias", [P, 1])
        cb, dtb, dpar = sb("cb", [P, HALF]), sb("dtb", [P, HALF]), sb("dpar", [P, HALF])
        rtw, rtb = sb("rtw", [P, NE]), sb("rtb", [1, NE])
        sel = sb("sel", [96, 2 * NS, P], BF16)
        tri, onesb = sb("tri", [P, P], BF16), sb("onesb", [P, P], BF16)
        eps_col = sb("eps_col", [P, 1])
        one_col = sb("one_col", [P, 1])
        xb = sb("xb", [P, 2, JT, DM])
        mv = sb("mv", [P, 2, JT, 2])
        r1 = sb("r1", [P, 2, JT])
        xs = sb("xs", [P, 2, HALF, L])
        sres = sb("sres", [P, 2, HALF, L])
        delta = sb("delta", [P, 2, HALF * L])
        du = sb("du", [P, 2, HALF, L])
        bcs = sb("bcs", [96, 2, L], BF16)
        st = sb("st", [P, JT, 6])
        lnv = sb("lnv", [P, JT])
        qv = sb("qv", [P, JT])
        r2 = sb("r2", [P, JT])
        r12 = sb("r12", [P, JT])
        hn = sb("hn", [P, JT, DM])
        hT = sb("hT", [P, L + TAPS - 1])
        dr = sb("dr", [P, L])
        bcr = sb("bcr", [96, L])
        bcm = sb("bcm", [96, L], BF16)
        zt = sb("zt", [P, HALF * L])
        az = sb("az", [P, HALF * L])
        dA = sb("dA", [P, 2, HALF * L])
        cs = sb("cs", [P, 2, L])
        hs = sb("hs", [P, 4, HALF * L])
        hc = sb("hc", [P, 2, HALF * L])
        y2 = sb("y2", [P, HALF * L])
        o = sb("o", [P, JT, DM])
        st2, mv2, lnv2, rr2 = (sb("st2", [P, JT, 6]), sb("mv2", [P, JT, 2]), sb("lnv2", [P, JT]),
                               sb("rr2", [P, JT]))
        st3, mv3, lnv3, rr3 = (sb("st3", [P, JT, 6]), sb("mv3", [P, JT, 2]), sb("lnv3", [P, JT]),
                               sb("rr3", [P, JT]))
        x1s = sb("x1s", [P, JT, DM])
        xn = sb("xn", [P, JT, DM])
        xnT = sb("xnT", [P, L])
        rest = sb("rest", [P, JT, DM])
        rows = sb("rows", [P, JT, ROW], BF16)
        lg = sb("lg", [P, JT, NE])
        top = sb("top", [P, JT, 8])
        topi = sb("topi", [P, JT, 8], U32)
        topf = sb("topf", [P, JT, TOPK])
        hot = sb("hot", [P, JT, TOPK, NE])
        picked = sb("picked", [P, JT, NE], BF16)
        dl, ex = sb("dl", [P, JT, TOPK]), sb("ex", [P, JT, TOPK])
        sm, rc = sb("sm", [P, JT]), sb("rc", [P, JT])
        pos = sb("pos", [P, JT, NE])
        hp = sb("hp", [P, JT, TOPK, NE])
        slf = sb("slf", [P, JT * TOPK])
        slu = sb("slu", [P, JT * TOPK], U32)
        idb = sb("idb", [P, JT], U32)

        pD = ctx.enter_context(nc.psum_tensor("pD", [P, 1024], F32))
        pY = [bank("pY0"), bank("pY1")]
        pB, pC, pP0, pP1 = bank("pB"), bank("pC"), bank("pP0"), bank("pP1")

        names = """w_in w_dve w_act w_pool x_in x1_ready x1_out
            pre var_ready r1_ready q_ready r2_ready h_ready hT_ps hT_ready xs_ps xs_ready res_ps
            sres_ready dr_ps bc_ps dr_ready hi_ready r_ready s_ready dt_ps z_ready ln_ready
            pre_act delta_ready du_ready
            b_ps c_ps da_ready cs_ready dbu_ready h_done hc_ready hc_used
            post y_evac y3_ready op_ps o_ready ov_ready or_ready xv_ready xr_ready xn_ready
            xnT_ps xnT_ready rhi_ready rr_ready rmid_ready rows_ready lg_ps lg_done m_ready
            d_ready ex_ready rk_ps rk_done slots_ready post_act sc_done meta passed""".split()
        s = {n: sem(n) for n in names}
        block = ctx.enter_context(nc.Block())
        S = s
        PRE, POST = 4 + 1 + 1 + 1 + 1 + 1, 22

        def schedule(eng, batch):
            batch(0, 0, False, True)
            with eng.Fori(0, NB // 2 - 1) as i:
                batch(i * 2 + 1, 1, True, True)
                batch(i * 2 + 2, 0, True, True)
            batch(NB - 1, 1, True, False)

        NW = 16

        @block.sync
        def _(sp):
            def load(dst, src, slow=False):
                sp.dma_start(dst, src, allow_slow_non_contiguous=slow).then_inc(S["w_in"], 16)

            def load_x(b, p):
                if not (isinstance(b, int) and b < 2):
                    sp.wait_ge(S["x1_ready"], b - 1)
                sp.dma_start(xb[:, p], x[bass.ds(b, 1)].rearrange("a (j p) c -> p (a j) c", p=P)
                             ).then_inc(S["x_in"], 16)

            def store_x1(b):
                sp.wait_ge(S["x1_ready"], b + 1)
                sp.dma_start(x1_d[bass.ds(b, 1)].rearrange("a (j p) c -> p (a j) c", p=P), x1s[:]
                             ).then_inc(S["x1_out"], 16)

            load_x(0, 0)
            load_x(1, 1)
            load(wx[:], in_w)
            load(cw[:], conv_w.rearrange("(o d) k -> o d k", o=1).to_broadcast([P, DI, TAPS]))
            load(xpw[:], xp_w.rearrange("(h p) n -> p h n", p=P))
            load(dtw[:], dt_w)
            load(ow[:], out_w.rearrange("(h p) n -> p h n", p=P))
            load(a_neg[:], a_log.rearrange("(h p) n -> p h n", p=P))
            load(nw[:], norm_w.rearrange("(p o) -> p o", o=1))
            load(nbias[:], norm_b.rearrange("(p o) -> p o", o=1))
            for dst, src in ((cb, conv_b), (dtb, dt_b), (dpar, d_par)):
                for h in range(HALF):
                    load(dst[:, h:h + 1], src[h * P:(h + 1) * P].rearrange("(p o) -> p o", o=1))
            load(rtw[:].rearrange("p (e o) -> p e o", o=1),
                 rt_w.rearrange("e (p o) -> p e o", o=1), slow=True)

            def batch(b, p, post, pre):
                if post:
                    store_x1(b - 1)
                    if pre:
                        load_x(b + 1, 1 - p)

            load(rtb[:], rt_b.rearrange("(o e) -> o e", o=1))
            schedule(sp, batch)
            store_x1(NB - 1)
            sp.wait_ge(S["x1_out"], NB * 16)

        @block.scalar
        def _(act):
            def pre_r1(b, p):
                act.wait_ge(S["var_ready"], b + 1)
                nc.scalar.activation(lnv[:], mv[:, p, :, 1], ACT.Ln, bias=eps_col[:]
                                     ).then_inc(S["pre_act"], 1)
                act.wait_ge(S["pre_act"], 6 * b + 1)
                nc.scalar.activation(r1[:, p], lnv[:], ACT.Exp, scale=-0.5
                                     ).then_inc(S["r1_ready"], 1)

            def pre_r2(b, p):
                act.wait_ge(S["q_ready"], b + 1)
                nc.scalar.activation(lnv[:], qv[:], ACT.Ln, bias=eps_col[:]
                                     ).then_inc(S["pre_act"], 1)
                act.wait_ge(S["pre_act"], 6 * b + 2)
                nc.scalar.activation(r2[:], lnv[:], ACT.Exp, scale=-0.5
                                     ).then_inc(S["r2_ready"], 1)

            def pre_hT(b, p):
                act.wait_ge(S["hT_ps"], b + 1)
                nc.scalar.activation(hT[:, TAPS - 1:], pP0[:], ACT.Identity, scale=nw[:],
                                     bias=nbias[:]).then_inc(S["hT_ready"], 1)

            def pre_silu(b, p):
                if not (isinstance(b, int) and b < 2):
                    act.wait_ge(S["y3_ready"], b - 1)
                for h in range(HALF):
                    act.wait_ge(S["xs_ps"], 2 * b + h + 1)
                    nc.scalar.activation(xs[:, p, h], (pP0, pP1)[h][:], ACT.Silu,
                                         bias=cb[:, h:h + 1]).then_inc(S["xs_ready"], 1)
                for h in range(HALF):
                    act.wait_ge(S["res_ps"], 2 * b + h + 1)
                    nc.scalar.activation(sres[:, p, h], (pP0, pP1)[h][:], ACT.Silu
                                         ).then_inc(S["sres_ready"], 1)

            def pre_dr(b, p):
                act.wait_ge(S["dr_ps"], b + 1)
                nc.scalar.activation(dr[:], pP0[:], ACT.Copy).then_inc(S["dr_ready"], 1)
                act.wait_ge(S["bc_ps"], b + 1)
                nc.scalar.activation(bcs[:, p], pP1[0:96, :], ACT.Copy
                                     ).then_inc(S["hi_ready"], 1)

            def pre_softplus(b, p):
                if not (isinstance(b, int) and b < 1):
                    act.wait_ge(S["delta_ready"], b)
                for h in range(HALF):
                    act.wait_ge(S["dt_ps"], 2 * b + h + 1)
                    nc.scalar.activation(zt[:, h * L:(h + 1) * L], (pP0, pP1)[h][:],
                                         ACT.Identity, bias=dtb[:, h:h + 1]
                                         ).then_inc(S["z_ready"], 1)
                act.wait_ge(S["z_ready"], 2 * b + 2)
                nc.scalar.activation(az[:], zt[:], ACT.Abs).then_inc(S["pre_act"], 1)
                act.wait_ge(S["pre_act"], 6 * b + 3)
                nc.scalar.activation(az[:], az[:], ACT.Exp, scale=-1.0
                                     ).then_inc(S["pre_act"], 1)
                act.wait_ge(S["pre_act"], 6 * b + 4)
                nc.scalar.activation(az[:], az[:], ACT.Ln, bias=one_col[:]
                                     ).then_inc(S["ln_ready"], 1)
                act.sem_inc(S["pre_act"], 2)

            def decay(b, p, n):
                g = b * NS + n
                if n == 0:
                    act.wait_ge(S["delta_ready"], b + 1)
                if not (isinstance(b, int) and g < 2):
                    act.wait_ge(S["h_done"], g - 1)
                buf = dA[:, n % 2]
                nc.scalar.activation(buf[:, 0:L], delta[:, p, 0:L], ACT.Exp,
                                     scale=a_neg[:, 0, n:n + 1])
                nc.scalar.activation(buf[:, L + 1:], delta[:, p, L + 1:], ACT.Exp,
                                     scale=a_neg[:, 1, n:n + 1]).then_inc(S["da_ready"], 1)
                act.wait_ge(S["c_ps"], g + 1)
                if not (isinstance(b, int) and g < 2):
                    act.wait_ge(S["hc_ready"], g - 1)
                nc.scalar.activation(cs[:, n % 2], pC[:], ACT.Copy).then_inc(S["cs_ready"], 1)

            def post_rstd(b, ready, v, l, r, done, k):
                act.wait_ge(ready, b + 1)
                nc.scalar.activation(l[:], v[:, :, 1], ACT.Ln, bias=eps_col[:]
                                     ).then_inc(S["post_act"], 1)
                act.wait_ge(S["post_act"], 2 * b + k)
                nc.scalar.activation(r[:], l[:], ACT.Exp, scale=-0.5).then_inc(done, 1)

            def post_xnT(b):
                act.wait_ge(S["xnT_ps"], b + 1)
                nc.scalar.activation(xnT[:], pP1[:], ACT.Copy).then_inc(S["xnT_ready"], 1)
                if not (isinstance(b, int) and b < 1):
                    act.wait_ge(S["sc_done"], b * 256)
                nc.scalar.activation(rows[:, :, 0:DM], xn[:], ACT.Copy
                                     ).then_inc(S["rhi_ready"], 1)

            def post_mid(b):
                act.wait_ge(S["rr_ready"], b + 1)
                nc.scalar.activation(rows[:, :, DM:2 * DM], rest[:], ACT.Copy
                                     ).then_inc(S["rmid_ready"], 1)

            def post_exp(b):
                act.wait_ge(S["d_ready"], b + 1)
                nc.scalar.activation(ex[:], dl[:], ACT.Exp).then_inc(S["ex_ready"], 1)

            def before(b, p, slot):
                if slot == 7:
                    pre_r1(b, p)
                elif slot == 8:
                    pre_r2(b, p)
                elif slot == 9:
                    pre_hT(b, p)
                elif slot == 11:
                    pre_silu(b, p)
                elif slot == 12:
                    pre_dr(b, p)
                elif slot == 14:
                    pre_softplus(b, p)

            def after(b, slot):
                if slot == 3:
                    post_rstd(b, S["ov_ready"], mv2, lnv2, rr2, S["or_ready"], 1)
                elif slot == 4:
                    post_rstd(b, S["xv_ready"], mv3, lnv3, rr3, S["xr_ready"], 2)
                elif slot == 5:
                    post_xnT(b)
                elif slot == 6:
                    post_mid(b)
                elif slot == 7:
                    post_exp(b)

            def batch(b, p, post, pre):
                for n in range(NS):
                    decay(b, p, n)
                    if post:
                        after(b - 1, n)
                    if pre:
                        before(b + 1, 1 - p, n)

            act.wait_ge(S["w_in"], NW * 16)
            nc.scalar.activation(a_neg[:], a_neg[:], ACT.Exp).then_inc(S["w_act"], 1)
            act.wait_ge(S["w_pool"], 12)
            act.wait_ge(S["w_dve"], 7)
            for slot in range(NS):
                before(0, 0, slot)
            schedule(act, batch)
            for slot in range(NS):
                after(NB - 1, slot)

        @block.gpsimd
        def _(pool):
            def scaled_state(b, n):
                g = b * NS + n
                pool.wait_ge(S["h_done"], g + 1)
                pool.wait_ge(S["cs_ready"], g + 1)
                if not (isinstance(b, int) and g < 2):
                    pool.wait_ge(S["hc_used"], g - 1)
                nc.gpsimd.tensor_tensor(
                    hc[:, n % 2].rearrange("p (h l) -> p h l", h=HALF),
                    hs[:, n % 4].rearrange("p (h l) -> p h l", h=HALF),
                    cs[:, n % 2].rearrange("p (o l) -> p o l", o=1).to_broadcast([P, HALF, L]),
                    ALU.mult).then_inc(S["hc_ready"], 1)

            def scatter(b, k):
                meta = rows[:].bitcast(U32)[:, :, ROW // 2 - 1]
                if k == 0:
                    pool.wait_ge(S["rows_ready"], b + 1)
                    pool.wait_ge(S["slots_ready"], b + 1)
                    if not (isinstance(b, int) and b < 1):
                        pool.wait_ge(S["meta"], b * 5)
                    pool.sem_inc(S["passed"], 1)
                    nc.gpsimd.tensor_copy(meta, idb[:]).then_inc(S["meta"], 1)
                else:
                    pool.wait_ge(S["sc_done"], b * 256 + 64 * k)
                    pool.sem_inc(S["passed"], 1)
                    nc.gpsimd.tensor_scalar(meta, meta, 1, None, ALU.add
                                            ).then_inc(S["meta"], 1)
                pool.wait_ge(S["meta"], b * 5 + k + 1)
                pool.sem_inc(S["passed"], 1)
                for j in range(JT):
                    c = j * TOPK + k
                    nc.gpsimd.indirect_dma_start(
                        rows_d, bass.IndirectOffsetOnAxis(ap=slu[:, c:c + 1], axis=0),
                        rows[:].bitcast(U32)[:, j, :], None).then_inc(S["sc_done"], 16)
                if k == TOPK - 1:
                    nc.gpsimd.tensor_scalar(idb[:], idb[:], TOPK * L, None, ALU.add
                                            ).then_inc(S["meta"], 1)

            def batch(b, p, post, pre):
                for n in range(NS):
                    scaled_state(b, n)
                    if post and n >= 9 and n % 2 == 1:
                        scatter(b - 1, (n - 9) // 2)

            nc.gpsimd.memset(sel[:], 0.0).then_inc(S["w_pool"], 1)
            nc.gpsimd.memset(tri[:], 0.0).then_inc(S["w_pool"], 1)
            nc.gpsimd.memset(onesb[:], 1.0).then_inc(S["w_pool"], 1)
            nc.gpsimd.memset(hT[:, 0:TAPS - 1], 0.0).then_inc(S["w_pool"], 1)
            nc.gpsimd.memset(eps_col[:], EPS).then_inc(S["w_pool"], 1)
            nc.gpsimd.memset(one_col[:], 1.0).then_inc(S["w_pool"], 1)
            nc.gpsimd.memset(dA[:], 0.0).then_inc(S["w_pool"], 1)
            nc.gpsimd.iota(idb[:], [[TOPK * P, JT]], base=0, channel_multiplier=TOPK
                           ).then_inc(S["w_pool"], 1)
            for part in range(3):
                pool.wait_ge(S["w_pool"], 8 + part)
                nc.gpsimd.affine_select(out=sel[:], in_=sel[:], compare_op=ALU.not_equal,
                                        fill=1.0, base=-32 * part, pattern=[[-1, 2 * NS], [0, P]],
                                        channel_multiplier=1).then_inc(S["w_pool"], 1)
            nc.gpsimd.affine_select(out=tri[:], in_=tri[:], compare_op=ALU.is_ge, fill=1.0,
                                    base=0, pattern=[[-1, P]], channel_multiplier=1
                                    ).then_inc(S["w_pool"], 1)
            pool.wait_ge(S["w_pool"], 12)
            schedule(pool, batch)
            for k in range(TOPK):
                scatter(NB - 1, k)
            pool.wait_ge(S["sc_done"], NB * 256)

        @block.vector
        def _(dve):
            def stats(src, sts, m, chain, at, done, b):
                for j in range(JT):
                    nc.vector.bn_stats(sts[:, j, :], src[:, j, :]).then_inc(chain, 1)
                dve.wait_ge(chain, at + JT)
                dve.sem_inc(S["passed"], 1)
                for j in range(JT):
                    last = nc.vector.bn_aggr(m[:, j, :], sts[:, j, :])
                last.then_inc(done, 1)

            def normal(dst, src, m, r, last_sem):
                for j in range(JT):
                    last = nc.vector.tensor_scalar(dst[:, j, :], src[:, j, :], m[:, j, 0:1],
                                                   r[:, j:j + 1], ALU.subtract, ALU.mult)
                last.then_inc(last_sem, 1)

            def pre_stats(b, p):
                dve.wait_ge(S["x_in"], b * 16 + 16)
                stats(xb[:, p], st, mv[:, p], S["pre"], b * PRE, S["var_ready"], b)

            def pre_q(b, p):
                dve.wait_ge(S["r1_ready"], b + 1)
                nc.vector.tensor_tensor(qv[:], mv[:, p, :, 1], r1[:, p], ALU.mult
                                        ).then_inc(S["pre"], 1)
                dve.wait_ge(S["pre"], b * PRE + 5)
                nc.vector.tensor_tensor(qv[:], qv[:], r1[:, p], ALU.mult
                                        ).then_inc(S["q_ready"], 1)

            def pre_norm(b, p):
                dve.wait_ge(S["r2_ready"], b + 1)
                nc.vector.tensor_tensor(r12[:], r1[:, p], r2[:], ALU.mult
                                        ).then_inc(S["pre"], 1)
                dve.wait_ge(S["pre"], b * PRE + 6)
                if not (isinstance(b, int) and b < 1):
                    dve.wait_ge(S["hT_ps"], b)
                normal(hn, xb[:, p], mv[:, p], r12, S["h_ready"])

            def pre_split(b, p):
                dve.wait_ge(S["hi_ready"], b + 1)
                nc.vector.tensor_tensor(bcr[:], pP1[0:96, :], bcs[:, p], ALU.subtract
                                        ).then_inc(S["r_ready"], 1)
                dve.wait_ge(S["r_ready"], b + 1)
                nc.vector.tensor_copy(bcs[32:64, p], bcr[32:64, :]).then_inc(S["pre"], 1)
                nc.vector.tensor_copy(bcm[64:96, :], bcr[64:96, :]).then_inc(S["pre"], 1)
                dve.wait_ge(S["pre"], b * PRE + 8)
                nc.vector.tensor_tensor(bcs[64:96, p], bcr[64:96, :], bcm[64:96, :],
                                        ALU.subtract).then_inc(S["s_ready"], 1)

            def pre_delta(b, p):
                dve.wait_ge(S["ln_ready"], b + 1)
                nc.vector.scalar_tensor_tensor(delta[:, p], zt[:], 0.0, az[:], ALU.max, ALU.add
                                               ).then_inc(S["delta_ready"], 1)
                dve.wait_ge(S["delta_ready"], b + 1)
                nc.vector.tensor_tensor(du[:, p].rearrange("p h l -> p (h l)"), delta[:, p],
                                        xs[:, p].rearrange("p h l -> p (h l)"), ALU.mult
                                        ).then_inc(S["du_ready"], 1)
                dve.sem_inc(S["pre"], 1)

            def recur(b, p, n):
                g = b * NS + n
                if n == 0:
                    dve.wait_ge(S["du_ready"], b + 1)
                dve.wait_ge(S["b_ps"], g + 1)
                if not (isinstance(b, int) and g < 1):
                    dve.wait_ge(S["h_done"], g)
                nc.vector.tensor_tensor(
                    pD[:].rearrange("p (h l) -> p h l", h=HALF), du[:, p],
                    pB[:].rearrange("p (o l) -> p o l", o=1).to_broadcast([P, HALF, L]),
                    ALU.mult).then_inc(S["dbu_ready"], 1)
                dve.wait_ge(S["dbu_ready"], g + 1)
                dve.wait_ge(S["da_ready"], g + 1)
                if not (isinstance(b, int) and g < 4):
                    dve.wait_ge(S["hc_ready"], g - 3)
                nc.vector.tensor_tensor_scan(hs[:, n % 4], dA[:, n % 2], pD[:], 0.0, ALU.mult,
                                             ALU.add).then_inc(S["h_done"], 1)

            def post_y(b, p):
                dve.wait_ge(S["hc_used"], (b + 1) * NS)
                if not (isinstance(b, int) and b < 1):
                    dve.wait_ge(S["op_ps"], b)
                for h in range(HALF):
                    last = nc.vector.scalar_tensor_tensor(
                        y2[:, h * L:(h + 1) * L], xs[:, p, h], dpar[:, h:h + 1], pY[h][:],
                        ALU.mult, ALU.add)
                last.then_inc(S["y_evac"], 1)
                dve.wait_ge(S["y_evac"], b + 1)
                nc.vector.tensor_tensor(y2[:], y2[:], sres[:, p].rearrange("p h l -> p (h l)"),
                                        ALU.mult).then_inc(S["y3_ready"], 1)

            def post_o(b, p):
                normal(o, xb[:, p], mv[:, p], r1[:, p], S["post"])
                dve.wait_ge(S["post"], b * POST + 1)
                dve.wait_ge(S["op_ps"], b + 1)
                nc.vector.tensor_tensor(o[:].rearrange("p j c -> p (j c)"),
                                        o[:].rearrange("p j c -> p (j c)"), pP0[:], ALU.add
                                        ).then_inc(S["o_ready"], 1)
                dve.wait_ge(S["o_ready"], b + 1)
                stats(o, st2, mv2, S["post"], b * POST + 1, S["ov_ready"], b)

            def post_x1(b, p):
                dve.wait_ge(S["or_ready"], b + 1)
                normal(o, o, mv2, rr2, S["post"])
                dve.wait_ge(S["post"], b * POST + 6)
                if not (isinstance(b, int) and b < 1):
                    dve.wait_ge(S["x1_out"], b * 16)
                nc.vector.tensor_tensor(x1s[:], o[:], xb[:, p], ALU.add
                                        ).then_inc(S["x1_ready"], 1)
                dve.wait_ge(S["x1_ready"], b + 1)
                stats(x1s, st3, mv3, S["post"], b * POST + 6, S["xv_ready"], b)

            def post_xn(b):
                dve.wait_ge(S["xr_ready"], b + 1)
                normal(xn, x1s, mv3, rr3, S["xn_ready"])

            def post_rest(b):
                dve.wait_ge(S["rhi_ready"], b + 1)
                nc.vector.tensor_tensor(rest[:], xn[:], rows[:, :, 0:DM], ALU.subtract
                                        ).then_inc(S["rr_ready"], 1)

            def post_top(b):
                dve.wait_ge(S["rmid_ready"], b + 1)
                nc.vector.tensor_tensor(rows[:, :, 2 * DM:3 * DM], rest[:],
                                        rows[:, :, DM:2 * DM], ALU.subtract
                                        ).then_inc(S["rows_ready"], 1)
                dve.wait_ge(S["lg_ps"], b + 1)
                nc.vector.tensor_copy(lg[:].rearrange("p j e -> p (j e)"), pP0[:, 0:JT * NE]
                                      ).then_inc(S["lg_done"], 1)
                dve.wait_ge(S["lg_done"], b + 1)
                dve.sem_inc(S["passed"], 1)
                for j in range(JT):
                    last = nc.vector.max(top[:, j], lg[:, j])
                last.then_inc(S["post"], 1)
                dve.wait_ge(S["post"], b * POST + 11)
                dve.sem_inc(S["passed"], 1)
                for j in range(JT):
                    last = nc.vector.max_index(topi[:, j], top[:, j], lg[:, j])
                last.then_inc(S["post"], 1)
                nc.vector.tensor_tensor(dl[:], top[:, :, 0:TOPK],
                                        top[:, :, 0:1].to_broadcast([P, JT, TOPK]), ALU.subtract
                                        ).then_inc(S["d_ready"], 1)
                dve.wait_ge(S["post"], b * POST + 12)
                nc.vector.tensor_copy(topf[:], topi[:, :, 0:TOPK]).then_inc(S["post"], 1)
                dve.wait_ge(S["post"], b * POST + 13)
                hotf = hot[:].rearrange("p j k e -> p (j k) e")
                nc.vector.tensor_tensor(
                    hotf, iota_e[:].rearrange("p (o e) -> p o e", o=1).to_broadcast(
                        [P, JT * TOPK, NE]),
                    topf[:].rearrange("p j (k o) -> p (j k) o", o=1).to_broadcast(
                        [P, JT * TOPK, NE]), ALU.is_equal).then_inc(S["post"], 1)
                dve.wait_ge(S["post"], b * POST + 14)
                with nc.allow_low_precision(reason="sums of at most one 1: exact in bf16"):
                    for j in range(JT):
                        last = nc.vector.tensor_reduce(picked[:, j],
                                                       hot[:, j].rearrange("p k e -> p e k"),
                                                       AX.X, ALU.add)
                last.then_inc(S["m_ready"], 1)

            def post_slots(b):
                dve.wait_ge(S["ex_ready"], b + 1)
                nc.vector.tensor_reduce(sm[:], ex[:], AX.X, ALU.add).then_inc(S["post"], 1)
                dve.wait_ge(S["post"], b * POST + 15)
                nc.vector.reciprocal(rc[:], sm[:]).then_inc(S["post"], 1)
                dve.wait_ge(S["post"], b * POST + 16)
                nc.vector.tensor_tensor(
                    keep["prob"][:, bass.ds(b * JT * TOPK, JT * TOPK)].rearrange(
                        "p (j k) -> p j k", k=TOPK), ex[:],
                    rc[:].rearrange("p (j o) -> p j o", o=1).to_broadcast([P, JT, TOPK]),
                    ALU.mult)
                dve.wait_ge(S["rk_ps"], b + 1)
                nc.vector.tensor_tensor(
                    pos[:], pP0[:, 0:JT * NE].rearrange("p (j e) -> p j e", e=NE),
                    base[:].rearrange("p (o e) -> p o e", o=1).to_broadcast([P, JT, NE]),
                    ALU.add).then_inc(S["post"], 1)
                dve.wait_ge(S["post"], b * POST + 17)
                nc.vector.tensor_tensor(base[:], base[:], pP0[:, JT * NE:(JT + 1) * NE], ALU.add
                                        ).then_inc(S["rk_done"], 1)
                for j in range(JT):
                    last = nc.vector.tensor_tensor(
                        hp[:, j], hot[:, j],
                        pos[:, j:j + 1].to_broadcast([P, TOPK, NE]), ALU.mult)
                last.then_inc(S["post"], 1)
                dve.wait_ge(S["post"], b * POST + 18)
                nc.vector.tensor_reduce(slf[:], hp[:].rearrange("p j k e -> p (j k) e"), AX.X,
                                        ALU.add).then_inc(S["post"], 1)
                dve.wait_ge(S["post"], b * POST + 19)
                if not (isinstance(b, int) and b < 1):
                    dve.wait_ge(S["sc_done"], b * 256)
                nc.vector.tensor_copy(slu[:], slf[:]).then_inc(S["slots_ready"], 1)
                dve.sem_inc(S["post"], POST - 19)

            def before(b, p, slot):
                if slot == 7:
                    pre_stats(b, p)
                elif slot == 8:
                    pre_q(b, p)
                elif slot == 9:
                    pre_norm(b, p)
                elif slot == 13:
                    pre_split(b, p)
                elif slot == 15:
                    pre_delta(b, p)

            def after(b, p, slot):
                if slot == 2:
                    post_y(b, p)
                elif slot == 3:
                    post_o(b, p)
                elif slot == 4:
                    post_x1(b, p)
                elif slot == 5:
                    post_xn(b)
                elif slot == 6:
                    post_rest(b)
                elif slot == 7:
                    post_top(b)
                elif slot == 8:
                    post_slots(b)

            def batch(b, p, post, pre):
                for n in range(NS):
                    recur(b, p, n)
                    if post:
                        after(b - 1, 1 - p, n)
                    if pre:
                        before(b + 1, 1 - p, n)

            dve.wait_ge(S["w_in"], NW * 16)
            dve.wait_ge(S["w_act"], 1)
            nc.vector.tensor_scalar(a_neg[:], a_neg[:], -1.0, None, ALU.mult
                                    ).then_inc(S["w_dve"], 1)
            for k in range(TAPS):
                nc.vector.tensor_tensor(wc[:, k], wx[:, 0:DI], cw[:, :, k], ALU.mult
                                        ).then_inc(S["w_dve"], 1)
            for h in range(HALF):
                nc.vector.tensor_copy(
                    xpw3[:, h], xpw[:, h:h + 1, P:].to_broadcast([P, 3, 2 * NS])
                    ).then_inc(S["w_dve"], 1)
            dve.wait_ge(S["w_pool"], 12)
            for slot in range(NS):
                before(0, 0, slot)
            schedule(dve, batch)
            for slot in range(NS):
                after(NB - 1, 1, slot)

        @block.tensor
        def _(pe):
            mm = nc.tensor.matmul

            def pre_hT(b, p):
                pe.wait_ge(S["h_ready"], b + 1)
                if not (isinstance(b, int) and b < 1):
                    pe.wait_ge(S["z_ready"], 2 * b)
                if not (isinstance(b, int) and b < 2):
                    pe.wait_ge(S["rk_done"], b - 1)
                for j in range(JT):
                    last = nc.tensor.transpose(pP0[:, j * P:(j + 1) * P], hn[:, j, :], ident[:])
                last.then_inc(S["hT_ps"], 1)

            def pre_in(b, p):
                pe.wait_ge(S["hT_ready"], b + 1)
                for h in range(HALF):
                    for k in range(TAPS):
                        last = mm((pP0, pP1)[h][:], wc[:, k, h * P:(h + 1) * P],
                                  hT[:, k:k + L], start=(k == 0), stop=(k == TAPS - 1))
                    last.then_inc(S["xs_ps"], 1)

            def pre_res(b, p):
                for h in range(HALF):
                    pe.wait_ge(S["xs_ready"], 2 * b + h + 1)
                    mm((pP0, pP1)[h][:], wx[:, DI + h * P:DI + (h + 1) * P],
                       hT[:, TAPS - 1:], start=True, stop=True).then_inc(S["res_ps"], 1)

            def pre_xp(b, p):
                pe.wait_ge(S["sres_ready"], 2 * b + 1)
                for h in range(HALF):
                    last = mm(pP0[:], xpw[:, h, 0:P], xs[:, p, h], start=(h == 0),
                              stop=(h == HALF - 1))
                last.then_inc(S["dr_ps"], 1)
                pe.wait_ge(S["sres_ready"], 2 * b + 2)
                for h in range(HALF):
                    last = mm(pP1[0:96, :], xpw3[:, h].rearrange("p t n -> p (t n)"),
                              xs[:, p, h], start=(h == 0), stop=(h == HALF - 1))
                last.then_inc(S["bc_ps"], 1)

            def pre_dt(b, p):
                pe.wait_ge(S["dr_ready"], b + 1)
                mm(pP0[:], dtw[:, 0:P], dr[:], start=True, stop=True).then_inc(S["dt_ps"], 1)
                pe.wait_ge(S["r_ready"], b + 1)
                mm(pP1[:], dtw[:, P:], dr[:], start=True, stop=True).then_inc(S["dt_ps"], 1)

            def spread(b, p, n):
                g = b * NS + n
                if n == 0:
                    pe.wait_ge(S["s_ready"], b + 1)
                if not (isinstance(b, int) and g < 1):
                    pe.wait_ge(S["dbu_ready"], g)
                mm(pB[:], sel[:, n, :], bcs[:, p], start=True, stop=True
                   ).then_inc(S["b_ps"], 1)
                if not (isinstance(b, int) and g < 1):
                    pe.wait_ge(S["cs_ready"], g)
                mm(pC[:], sel[:, NS + n, :], bcs[:, p], start=True, stop=True
                   ).then_inc(S["c_ps"], 1)

            def gather_state(b, n):
                g = b * NS + n
                pe.wait_ge(S["hc_ready"], g + 1)
                if n == 0 and not (isinstance(b, int) and b < 1):
                    pe.wait_ge(S["y_evac"], b)
                for h in range(HALF):
                    last = mm(pY[h][:], ident[:], hc[:, n % 2, h * L:(h + 1) * L],
                              start=(n == 0), stop=(n == NS - 1))
                last.then_inc(S["hc_used"], 1)

            def post_out(b, done):
                pe.wait_ge(S["y3_ready"], b + 1)
                pe.wait_ge(S["z_ready"], done)
                for j in range(JT):
                    for h in range(HALF):
                        last = mm(pP0[:, j * DM:(j + 1) * DM],
                                  y2[:, h * L + j * P:h * L + (j + 1) * P], ow[:, h],
                                  start=(h == 0), stop=(h == HALF - 1))
                last.then_inc(S["op_ps"], 1)

            def post_xnT(b):
                pe.wait_ge(S["xn_ready"], b + 1)
                for j in range(JT):
                    last = nc.tensor.transpose(pP1[:, j * P:(j + 1) * P], xn[:, j, :], ident[:])
                last.then_inc(S["xnT_ps"], 1)

            def post_logits(b):
                pe.wait_ge(S["xnT_ready"], b + 1)
                pe.wait_ge(S["o_ready"], b + 1)
                for j in range(JT):
                    mm(pP0[:, j * NE:(j + 1) * NE], xnT[:, j * P:(j + 1) * P], rtw[:],
                       start=True, stop=False)
                    last = mm(pP0[:, j * NE:(j + 1) * NE], keep["ones_row"][:], rtb[:],
                              start=False, stop=True)
                last.then_inc(S["lg_ps"], 1)

            def post_rank(b):
                pe.wait_ge(S["m_ready"], b + 1)
                pe.wait_ge(S["lg_done"], b + 1)
                for j in range(JT):
                    for i in range(j + 1):
                        mm(pP0[:, j * NE:(j + 1) * NE], (tri if i == j else onesb)[:],
                           picked[:, i], start=(i == 0), stop=(i == j))
                for i in range(JT):
                    last = mm(pP0[:, JT * NE:(JT + 1) * NE], onesb[:], picked[:, i],
                              start=(i == 0), stop=(i == JT - 1))
                last.then_inc(S["rk_ps"], 1)

            def before(b, p, slot):
                if slot == 9:
                    pre_hT(b, p)
                elif slot == 10:
                    pre_in(b, p)
                elif slot == 11:
                    pre_res(b, p)
                elif slot == 12:
                    pre_xp(b, p)
                elif slot == 13:
                    pre_dt(b, p)

            def after(b, slot, done):
                if slot == 2:
                    post_out(b, done)
                elif slot == 5:
                    post_xnT(b)
                elif slot == 6:
                    post_logits(b)
                elif slot == 7:
                    post_rank(b)

            def batch(b, p, post, pre):
                for n in range(NS):
                    spread(b, p, n)
                    if n >= 2:
                        gather_state(b, n - 2)
                    elif post:
                        gather_state(b - 1, NS - 2 + n)
                    if post:
                        after(b - 1, n, 2 * b + 2)
                    if pre:
                        before(b + 1, 1 - p, n)

            pe.wait_ge(S["w_dve"], 7)
            pe.wait_ge(S["w_pool"], 12)
            for slot in range(NS):
                before(0, 0, slot)
            schedule(pe, batch)
            gather_state(NB - 1, NS - 2)
            gather_state(NB - 1, NS - 1)
            for slot in range(NS):
                after(NB - 1, slot, 2 * NB)


def expert_phase(nc, keep, rows_d, yk_d):
    identb, w_all, wd32 = keep["identb"], keep["w_all"], keep["wd32"]
    RING = 4
    with ExitStack() as ctx:
        def sb(name, shape, dt=F32):
            return ctx.enter_context(nc.sbuf_tensor(name, shape, dt))

        def bank(name, dt=F32):
            return ctx.enter_context(nc.psum_tensor(name, [P, 2048 // (4 if dt == F32 else 2)],
                                                    dt))

        def sem(name):
            return ctx.enter_context(nc.semaphore(name))

        cnt = sb("cnt", [1, NE])
        cnti = sb("cnti", [1, NE], I32)
        ntile = sb("ntile", [1, NE])
        cum = sb("cum", [1, NE])
        ones_e = sb("ones_e", [1, NE])
        first = sb("first", [1, NE])
        ti = sb("ti", [1, NT])
        cmp = sb("cmp", [1, NT, NE])
        ef = sb("ef", [1, NT])
        valid = sb("valid", [1, NT])
        rowf = sb("rowf", [1, NT])
        tab_e = sb("tab_e", [1, NT], I32)
        tab_r = sb("tab_r", [1, NT], I32)
        endi = sb("endi", [1, NE], I32)
        pad = sb("pad", [P, 2, ROW], BF16)
        xr = sb("xr", [P, RING, 2, ROW], BF16)
        xT = sb("xT", [P, 2, 3 * TILE], BF16)
        gt = sb("gt", [P, 2, FH * TILE])
        sg = sb("sg", [P, 2, FH * TILE])
        ut = sb("ut", [P, 2, FH * TILE])
        it = sb("it", [P, 2, FH * TILE])
        yo = sb("yo", [P, 2, 2, DM])
        pX = [bank(f"pX{i}", BF16) for i in range(2)]
        pG = [bank(f"pG{i}") for i in range(2)]
        pU = [bank(f"pU{i}") for i in range(2)]
        pO = [bank(f"pO{i}") for i in range(2)]
        padded, pad_made, t_link, table_ready, xT_ps, xT_ready, g_ps, u_ps = (
            sem(n) for n in ("padded", "pad_made", "t_link", "table_ready", "xT_ps", "xT_ready",
                             "g_ps", "u_ps"))
        g_ready, u_ready, sg_ready, glu_ready, it_ready, o_ps, y_ready, e_passed = (
            sem(n) for n in ("g_ready", "u_ready", "sg_ready", "glu_ready", "it_ready", "o_ps",
                             "y_ready", "e_passed"))
        rows_in = [sem(f"rows_in{r}") for r in range(RING)]
        y_out = [sem(f"y_out{q}") for q in range(2)]
        block = ctx.enter_context(nc.Block())

        def schedule(eng, tile):
            for t in range(RING):
                tile(t, t)
            with eng.Fori(1, NT // RING - 1) as i:
                for u in range(RING):
                    tile(i * RING + u, u)
            for t in range(NT - RING, NT):
                tile(t, t % RING)

        def early(t, k):
            return isinstance(t, int) and t < k

        def scattered(t, u):
            if isinstance(t, int):
                return 32 * (t // 2 + 1)
            return (t - u % 2) * 16 + 32

        @block.sync
        def _(sp):
            def tile(t, u):
                row = sp.value_load(tab_r[0:1, bass.ds(t, 1)], min_val=0, max_val=NE * REGION)
                if not early(t, RING):
                    sp.wait_ge(y_out[u % 2], scattered(t - RING, u))
                sp.dma_start(xr[:].bitcast(U32)[:, u], rows_d[bass.ds(row, TILE), :].rearrange(
                    "(p s) c -> p s c", s=2)).then_inc(rows_in[u], 16)

            sp.wait_ge(pad_made, 2)
            sp.wait_ge(table_ready, 1)
            with sp.Fori(0, NE) as e:
                end = sp.value_load(endi[0:1, bass.ds(e, 1)], min_val=0,
                                    max_val=NE * REGION - TILE)
                sp.dma_start(rows_d[bass.ds(end, TILE), :].rearrange("(p s) c -> p s c", s=2),
                             pad[:].bitcast(U32)).then_inc(padded, 16)
            sp.dma_start(rows_d[NE * REGION:NE * REGION + TILE, :].rearrange(
                "(p s) c -> p s c", s=2), pad[:].bitcast(U32)).then_inc(padded, 16)
            sp.wait_ge(padded, (NE + 1) * 16)
            sp.wait_ge(table_ready, 2)
            schedule(sp, tile)

        @block.gpsimd
        def _(pool):
            nc.gpsimd.memset(pad[:, :, 0:3 * DM], 0.0).then_inc(pad_made, 1)
            nc.gpsimd.iota(pad[:].bitcast(U32)[:, :, ROW // 2 - 1], [[0, 2]], base=NO_TOKEN,
                           channel_multiplier=0).then_inc(pad_made, 1)
            nc.gpsimd.iota(ti[:], [[1, NT]], base=0, channel_multiplier=0,
                           allow_small_or_imprecise_dtypes=True).then_inc(pad_made, 1)
            nc.gpsimd.memset(ones_e[:], 1.0).then_inc(pad_made, 1)

            def tile(t, u):
                pool.wait_ge(y_ready, t + 1)
                pool.sem_inc(e_passed, 1)
                ids = xr[:].bitcast(U32)
                for sx in range(2):
                    nc.gpsimd.indirect_dma_start(
                        yk_d, bass.IndirectOffsetOnAxis(ap=ids[:, u, sx, ROW // 2 - 1:ROW // 2],
                                                        axis=0),
                        yo[:, u % 2, sx, :], None, bounds_check=TOKENS * TOPK - 1,
                        oob_is_err=False).then_inc(y_out[u % 2], 16)

            schedule(pool, tile)
            for q in range(2):
                pool.wait_ge(y_out[q], 16 * NT)

        @block.scalar
        def _(act):
            def evac_x(t, q):
                act.wait_ge(xT_ps, t + 1)
                nc.scalar.activation(xT[:, q], pX[q][:, 0:3 * TILE], ACT.Copy
                                     ).then_inc(xT_ready, 1)

            def evac_y(t, q, u):
                act.wait_ge(o_ps, t + 1)
                if not early(t, 2):
                    act.wait_ge(y_out[q], scattered(t - 2, u))
                nc.scalar.activation(yo[:, q].rearrange("p s c -> p (s c)"),
                                     pO[q][:, 0:2 * DM], ACT.Copy).then_inc(y_ready, 1)

            def tile(t, u):
                q = u % 2
                act.wait_ge(g_ready, t + 1)
                if not early(t, 2):
                    act.wait_ge(glu_ready, t - 1)
                nc.scalar.activation(sg[:, q], gt[:, q], ACT.Sigmoid, scale=SIG_SCALE
                                     ).then_inc(sg_ready, 1)
                if not (isinstance(t, int) and t == NT - 1):
                    evac_x(t + 1, 1 - q)
                if not early(t, 1):
                    evac_y(t - 1, 1 - q, u - 1)

            evac_x(0, 0)
            schedule(act, tile)
            evac_y(NT - 1, 1, NT - 1)

        @block.vector
        def _(dve):
            dve.wait_ge(pad_made, 4)
            nc.vector.tensor_copy(endi[:], keep["base"][0:1, :]).then_inc(table_ready, 1)
            link = [0]

            def chain(ins):
                link[0] += 1
                ins.then_inc(t_link, 1)
                dve.wait_ge(t_link, link[0])

            chain(nc.vector.tensor_tensor(cnt[:], keep["base"][0:1, :], keep["ebase"][0:1, :],
                                          ALU.subtract))
            chain(nc.vector.tensor_scalar(cnti[:], cnt[:], float(TILE - 1), None, ALU.add))
            chain(nc.vector.tensor_scalar(cnti[:], cnti[:], 8, None, ALU.logical_shift_right))
            chain(nc.vector.tensor_copy(ntile[:], cnti[:]))
            chain(nc.vector.tensor_tensor_scan(cum[:], ones_e[:], ntile[:], 0.0, ALU.mult,
                                               ALU.add))
            chain(nc.vector.tensor_tensor(first[:], cum[:], ntile[:], ALU.subtract))
            chain(nc.vector.scalar_tensor_tensor(first[:], first[:], -float(TILE),
                                                 keep["ebase"][0:1, :], ALU.mult, ALU.add))
            wide = [1, NT, NE]
            t_w = ti[:].rearrange("p (t o) -> p t o", o=1).to_broadcast(wide)
            chain(nc.vector.tensor_tensor(
                cmp[:], t_w, cum[:].rearrange("p (o e) -> p o e", o=1).to_broadcast(wide),
                ALU.is_ge))
            chain(nc.vector.tensor_reduce(ef[:], cmp[:], AX.X, ALU.add))
            chain(nc.vector.tensor_scalar(valid[:], ef[:], float(NE), None, ALU.is_lt))
            chain(nc.vector.tensor_tensor(
                cmp[:], ef[:].rearrange("p (t o) -> p t o", o=1).to_broadcast(wide),
                keep["iota_e"][0:1, :].rearrange("p (o e) -> p o e", o=1).to_broadcast(wide),
                ALU.is_equal))
            chain(nc.vector.tensor_tensor(
                cmp[:], cmp[:], first[:].rearrange("p (o e) -> p o e", o=1).to_broadcast(wide),
                ALU.mult))
            chain(nc.vector.tensor_reduce(rowf[:], cmp[:], AX.X, ALU.add))
            chain(nc.vector.tensor_scalar(ti[:], ti[:], float(TILE), -float(NE * REGION),
                                          ALU.mult, ALU.add))
            chain(nc.vector.tensor_tensor(ti[:], ti[:], valid[:], ALU.mult))
            chain(nc.vector.scalar_tensor_tensor(rowf[:], rowf[:], float(NE * REGION), ti[:],
                                                 ALU.add, ALU.add))
            chain(nc.vector.tensor_scalar(tab_e[:], ef[:], float(NE - 1), None, ALU.min))
            nc.vector.tensor_copy(tab_r[:], rowf[:]).then_inc(table_ready, 1)

            def tile(t, u):
                q = u % 2
                e = dve.value_load(tab_e[0:1, bass.ds(t, 1)], min_val=0, max_val=NE - 1)
                dve.wait_ge(g_ps, t + 1)
                if not early(t, 2):
                    dve.wait_ge(sg_ready, t - 1)
                dve.sem_inc(e_passed, 1)
                for h in range(FH):
                    last = nc.vector.tensor_scalar(
                        gt[:, q, h * TILE:(h + 1) * TILE], pG[q][:, h * TILE:(h + 1) * TILE],
                        keep["bg"][:, bass.ds(e * FH + h, 1)], GATE_MAX, ALU.add, ALU.min)
                last.then_inc(g_ready, 1)
                dve.wait_ge(u_ps, t + 1)
                dve.sem_inc(e_passed, 1)
                for h in range(FH):
                    last = nc.vector.tensor_scalar(
                        ut[:, q, h * TILE:(h + 1) * TILE], pU[q][:, h * TILE:(h + 1) * TILE],
                        keep["bu"][:, bass.ds(e * FH + h, 1)], GATE_MAX + 1.0, ALU.add, ALU.min)
                last.then_inc(u_ready, 1)
                dve.wait_ge(sg_ready, t + 1)
                nc.vector.tensor_tensor(gt[:, q], gt[:, q], sg[:, q], ALU.mult
                                        ).then_inc(glu_ready, 1)
                dve.wait_ge(glu_ready, t + 1)
                dve.wait_ge(u_ready, t + 1)
                if not early(t, 2):
                    dve.wait_ge(o_ps, t - 1)
                nc.vector.scalar_tensor_tensor(it[:, q], ut[:, q], 1.0 - GATE_MAX, gt[:, q],
                                               ALU.max, ALU.mult).then_inc(it_ready, 1)

            schedule(dve, tile)

        @block.tensor
        def _(pe):
            mm = nc.tensor.matmul

            def turn(t, q, r, turns):
                pe.wait_ge(rows_in[r], turns)
                if not early(t, 2):
                    pe.wait_ge(xT_ready, t - 1)
                for part in range(3):
                    for sx in range(2):
                        at = (part * 2 + sx) * P
                        last = nc.tensor.transpose(pX[q][:, at:at + P],
                                                   xr[:, r, sx, part * DM:(part + 1) * DM],
                                                   identb[:])
                last.then_inc(xT_ps, 1)

            def gate_up(t, q):
                e = pe.value_load(tab_e[0:1, bass.ds(t, 1)], min_val=0, max_val=NE - 1)
                pe.wait_ge(xT_ready, t + 1)
                for m, (ps, done, left) in enumerate(((pG, g_ps, g_ready), (pU, u_ps, u_ready))):
                    if not early(t, 2):
                        pe.wait_ge(left, t - 1)
                    pe.sem_inc(e_passed, 1)
                    for h in range(FH):
                        for part in range(3):
                            last = mm(ps[q][:, h * TILE:(h + 1) * TILE],
                                      w_all[:, bass.ds(m * 4 * CW + (e * FH + h) * P, P)],
                                      xT[:, q, part * TILE:(part + 1) * TILE],
                                      start=(part == 0), stop=(part == 2))
                    last.then_inc(done, 1)

            def down(t, q):
                e = pe.value_load(tab_e[0:1, bass.ds(t, 1)], min_val=0, max_val=NE - 1)
                pe.wait_ge(it_ready, t + 1)
                if not early(t, 2):
                    pe.wait_ge(y_ready, t - 1)
                pe.sem_inc(e_passed, 1)
                for sx in range(2):
                    for h in range(FH):
                        mm(pO[q][:, sx * DM:(sx + 1) * DM],
                           it[:, q, h * TILE + sx * P:h * TILE + (sx + 1) * P],
                           wd32[:, bass.ds((e * FH + h) * DM, DM)], start=(h == 0), stop=False)
                    last = mm(pO[q][:, sx * DM:(sx + 1) * DM], keep["ones_row"][:],
                              keep["bd"][0:1, bass.ds(e * DM, DM)], start=False, stop=True)
                last.then_inc(o_ps, 1)

            def tile(t, u):
                q = u % 2
                gate_up(t, q)
                if not (isinstance(t, int) and t == NT - 1):
                    r = (u + 1) % RING
                    turns = (16 * ((t + 1) // RING + 1) if isinstance(t, int)
                             else (t + 1 - r) * (16 // RING) + 16)
                    turn(t + 1, 1 - q, r, turns)
                if not early(t, 1):
                    down(t - 1, 1 - q)

            pe.wait_ge(table_ready, 2)
            turn(0, 0, 0, 16)
            schedule(pe, tile)
            down(NT - 1, 1)


def combine_phase(nc, keep, yk_d, x1_d, out):
    with ExitStack() as ctx:
        def sb(name, shape, dt=F32):
            return ctx.enter_context(nc.sbuf_tensor(name, shape, dt))

        def sem(name):
            return ctx.enter_context(nc.semaphore(name))

        yk = sb("yk", [P, 2, JT * TOPK, DM])
        xm = sb("xm", [P, 2, JT, DM])
        mo = sb("mo", [P, 2, JT, DM])
        wt = sb("wt", [P, 2, JT * TOPK, DM])
        res = sb("res", [P, 2, JT, DM])
        st = sb("stc", [P, JT, 6])
        mv = sb("mvc", [P, JT, 2])
        lnv, rr = sb("lnvc", [P, JT]), sb("rrc", [P, JT])
        eps = sb("epsc", [P, 1])
        yk_in = [sem(f"yk_in{q}") for q in range(2)]
        xm_in = [sem(f"xm_in{q}") for q in range(2)]
        eps_made, wt_ready, mo_ready, link, v_ready, r_ready, res_ready, a_link, passed2 = (
            sem(n) for n in ("eps_made", "wt_ready", "mo_ready", "clink", "cv_ready",
                             "cr_ready", "res_ready", "a_link", "passed2"))
        stored = [sem(f"cstored{q}") for q in range(2)]
        block = ctx.enter_context(nc.Block())

        def schedule(eng, step):
            step(0, 0)
            step(1, 1)
            with eng.Fori(1, NB // 2) as i:
                step(i * 2, 0)
                step(i * 2 + 1, 1)

        def early(c, k):
            return isinstance(c, int) and c < k

        @block.sync
        def _(sp):
            def step(c, q):
                if not early(c, 2):
                    sp.wait_ge(wt_ready, c - 1)
                    sp.wait_ge(res_ready, c - 1)
                sp.dma_start(yk[:, q].rearrange("p (j k) c -> p j (k c)", k=TOPK),
                             yk_d[bass.ds(c * L * TOPK, L * TOPK), :].rearrange(
                                 "(j p k) c -> p j (k c)", p=P, k=TOPK)).then_inc(yk_in[q], 16)
                sp.dma_start(xm[:, q], x1_d[bass.ds(c, 1)].rearrange(
                    "a (j p) c -> p (a j) c", p=P)).then_inc(xm_in[q], 16)

            schedule(sp, step)

        @block.gpsimd
        def _(pool):
            nc.gpsimd.memset(eps[:], EPS).then_inc(eps_made, 1)

            def step(c, q):
                n = 16 * (c // 2 + 1) if isinstance(c, int) else (c - q) * 8 + 16
                pool.wait_ge(yk_in[q], n)
                if not early(c, 2):
                    pool.wait_ge(mo_ready, c - 1)
                pool.sem_inc(passed2, 1)
                nc.gpsimd.tensor_tensor(
                    wt[:, q], yk[:, q],
                    keep["prob"][:, bass.ds(c * JT * TOPK, JT * TOPK)].rearrange(
                        "p (g o) -> p g o", o=1).to_broadcast([P, JT * TOPK, DM]),
                    ALU.mult).then_inc(wt_ready, 1)

            schedule(pool, step)

        @block.scalar
        def _(act):
            def step(c, q):
                act.wait_ge(v_ready, c + 1)
                nc.scalar.activation(lnv[:], mv[:, :, 1], ACT.Ln, bias=eps[:]
                                     ).then_inc(a_link, 1)
                act.wait_ge(a_link, c + 1)
                nc.scalar.activation(rr[:], lnv[:], ACT.Exp, scale=-0.5).then_inc(r_ready, 1)
                act.wait_ge(res_ready, c + 1)
                act.dma_start(out[bass.ds(c, 1)].rearrange("a (j p) c -> p (a j) c", p=P),
                              res[:, q]).then_inc(stored[q], 16)

            act.wait_ge(eps_made, 1)
            schedule(act, step)
            for q in range(2):
                act.wait_ge(stored[q], NB * 8)

        @block.vector
        def _(dve):
            def step(c, q):
                n = 16 * (c // 2 + 1) if isinstance(c, int) else (c - q) * 8 + 16
                dve.wait_ge(wt_ready, c + 1)
                for j in range(JT):
                    last = nc.vector.tensor_reduce(
                        mo[:, q, j], wt[:, q, j * TOPK:(j + 1) * TOPK].rearrange(
                            "p k c -> p c k"), AX.X, ALU.add)
                last.then_inc(mo_ready, 1)
                dve.wait_ge(mo_ready, c + 1)
                for j in range(JT):
                    last = nc.vector.bn_stats(st[:, j, :], mo[:, q, j])
                last.then_inc(link, 1)
                dve.wait_ge(link, 2 * c + 1)
                dve.sem_inc(passed2, 1)
                for j in range(JT):
                    last = nc.vector.bn_aggr(mv[:, j, :], st[:, j, :])
                last.then_inc(v_ready, 1)
                dve.wait_ge(r_ready, c + 1)
                for j in range(JT):
                    last = nc.vector.tensor_scalar(mo[:, q, j], mo[:, q, j], mv[:, j, 0:1],
                                                   rr[:, j:j + 1], ALU.subtract, ALU.mult)
                last.then_inc(link, 1)
                dve.wait_ge(link, 2 * c + 2)
                dve.wait_ge(xm_in[q], n)
                if not early(c, 2):
                    dve.wait_ge(stored[q], n - 16)
                nc.vector.tensor_tensor(res[:, q], mo[:, q], xm[:, q], ALU.add
                                        ).then_inc(res_ready, 1)

            schedule(dve, step)


_INS = ['L0_attn_x', 'L0_attn_norm_w', 'L0_attn_norm_b', 'L0_attn_in_proj_w', 'L0_attn_conv_w',
        'L0_attn_conv_b', 'L0_attn_x_proj_w', 'L0_attn_dt_proj_w', 'L0_attn_dt_proj_b',
        'L0_attn_A_log', 'L0_attn_D_param', 'L0_attn_out_proj_w', 'L0_ffn_router_weight',
        'L0_ffn_router_bias', 'L0_ffn_gate_proj_bias', 'L0_ffn_up_proj_bias',
        'L0_ffn_down_proj_bias', 'L0_ffn_gate_proj_blocks', 'L0_ffn_gate_proj_scales',
        'L0_ffn_up_proj_blocks', 'L0_ffn_up_proj_scales', 'L0_ffn_down_proj_blocks',
        'L0_ffn_down_proj_scales']
_OUTS = [((NB, L, DM), 'float32')]


def kernel(**inputs):
    import numpy as _np
    import concourse.bacc as _bacc
    from concourse import mybir as _mybir
    from concourse.bass_utils import run_bass_kernel_spmd as _run

    nc = _bacc.Bacc("TRN2", target_bir_lowering=False, num_devices=1)
    arrays, args = {}, []
    for name in _INS:
        a = _np.ascontiguousarray(inputs[name])
        if a.dtype == _np.uint8:
            a = a.view(_np.uint32)
        arrays[f"in_{name}_dram"] = a
        args.append(nc.dram_tensor(f"in_{name}_dram", a.shape, _mybir.dt.from_np(a.dtype),
                                   kind="ExternalInput").ap())
    for i, (shape, dtype) in enumerate(_OUTS):
        dt = _mybir.dt.from_np(_np.dtype(dtype))
        args.append(nc.dram_tensor(f"out_{i}_dram", shape, dt, kind="ExternalOutput").ap())
    build(nc, *args)
    r = _run(nc, [arrays], core_ids=[0])
    return r.results[0]["out_0_dram"]
```

```python
from contextlib import ExitStack

import concourse.bass as bass
from concourse import mybir

F32, BF16, I32, U32, U8 = (mybir.dt.float32, mybir.dt.bfloat16, mybir.dt.int32,
                           mybir.dt.uint32, mybir.dt.uint8)
F8 = mybir.dt.float8e4
ALU = mybir.AluOpType
ACT = mybir.ActivationFunctionType
AX = mybir.AxisListType

P = 128
NB, L, DM = 16, 512, 128
DI, NS, TAPS = 256, 16, 4
HALF = DI // P
JT = L // P
TOKENS = NB * L
NE, FI, TOPK = 16, 256, 4
FH = FI // P
EPS = 1e-5
GATE_MAX, SIG_SCALE = 7.0, 1.702
TILE = 256
REGION = TOKENS + TILE
NT = TOKENS * TOPK // TILE + NE
ROW = 3 * DM + 4
ID, WEIGHT = 3 * DM // 2, 3 * DM // 2 + 1
NO_TOKEN = 1 << 20
CHUNKS, CW = 12, 1024


def build(nc, x, norm_w, norm_b, in_w, conv_w, conv_b, xp_w, dt_w, dt_b, a_log, d_par, out_w,
          rt_w, rt_b, g_bias, u_bias, d_bias, g_blk, g_scl, u_blk, u_scl, d_blk, d_scl, out):
    rows_d = nc.dram_tensor("expert_rows", ((NE + 1) * REGION, ROW // 2), U32).ap()
    yk_d = nc.dram_tensor("expert_out", (TOKENS * TOPK, DM), F32).ap()
    x1_d = nc.dram_tensor("x_mid", (NB, L, DM), F32).ap()
    with ExitStack() as ctx:
        def sb(name, shape, dt=F32):
            return ctx.enter_context(nc.sbuf_tensor(name, shape, dt))
        keep = dict(
            ident=sb("ident", [P, P]), identb=sb("identb", [P, P], BF16),
            w_all=sb("w_all", [P, CHUNKS * CW], BF16),
            bg=sb("bg", [P, NE * FH]), bu=sb("bu", [P, NE * FH]),
            ones_row=sb("ones_row", [1, P]),
            base=sb("base", [P, NE]), ebase=sb("ebase", [P, NE]), iota_e=sb("iota_e", [P, NE]),
        )
        setup_phase(nc, keep, g_blk, g_scl, u_blk, u_scl, d_blk, d_scl, g_bias, u_bias)
        mamba_phase(nc, keep, x, norm_w, norm_b, in_w, conv_w, conv_b, xp_w, dt_w, dt_b, a_log,
                    d_par, out_w, rt_w, rt_b, rows_d, x1_d)
        expert_phase(nc, keep, d_bias, rows_d, yk_d)
        combine_phase(nc, keep, yk_d, x1_d, out)


def setup_phase(nc, keep, g_blk, g_scl, u_blk, u_scl, d_blk, d_scl, g_bias, u_bias):
    ident, identb, w_all = keep["ident"], keep["identb"], keep["w_all"]
    with ExitStack() as ctx:
        def sb(name, shape, dt=F32):
            return ctx.enter_context(nc.sbuf_tensor(name, shape, dt))

        def sem(name):
            return ctx.enter_context(nc.semaphore(name))

        CB = CW // 2
        codes = sb("codes", [P, CHUNKS * CB], U8)
        scl8 = sb("scl8", [P, CHUNKS * 32], U8)
        codes_w, scl_w = codes[:].bitcast(U32), scl8[:].bitcast(U32)
        scl32 = sb("scl32", [P, CHUNKS * 32], I32)
        part = sb("part", [P, 4, CB], U32)
        lo8, hi8 = sb("lo8", [P, CHUNKS * CB], U8), sb("hi8", [P, CHUNKS * CB], U8)
        wq = sb("wq", [P, 2, CW], BF16)
        wps = [ctx.enter_context(nc.psum_tensor(f"wps{i}", [P, CW], BF16)) for i in range(2)]
        loaded, loaded_g, loaded_u, loaded_d, made, link, quant, turned, stored = (
            sem(n) for n in ("loaded", "loaded_g", "loaded_u", "loaded_d", "made", "link",
                             "quant", "turned", "stored"))
        LOADS = (4, 4, 2)
        block = ctx.enter_context(nc.Block())

        @block.sync
        def _(sp):
            for m, (blk, scl, done) in enumerate(((g_blk, g_scl, loaded_g),
                                                  (u_blk, u_scl, loaded_u))):
                for h in range(FH):
                    dst = codes_w[:, m * CB:(m + 1) * CB].rearrange(
                        "p (e h c) -> p e h c", e=NE, h=FH)[:, :, h, :]
                    sp.dma_start(dst, blk[:, h * P:(h + 1) * P, :].rearrange("e p c -> p e c")
                                 ).then_inc(done, 16)
                    dst = scl_w[:, m * 32:(m + 1) * 32].rearrange(
                        "p (e h c) -> p e h c", e=NE, h=FH)[:, :, h, :]
                    sp.dma_start(dst, scl[:, h * P:(h + 1) * P, :].rearrange("e p c -> p e c"),
                                 allow_slow_non_contiguous=True).then_inc(done, 16)
            sp.dma_start(codes_w[:, 2 * CB:].rearrange("p (e c) -> p e c", e=NE),
                         d_blk.rearrange("e p c -> p e c")).then_inc(loaded_d, 16)
            sp.dma_start(scl_w[:, 64:].rearrange("p (e c) -> p e c", e=NE),
                         d_scl.rearrange("e p c -> p e c")).then_inc(loaded_d, 16)
            for dst, src in ((keep["bg"], g_bias), (keep["bu"], u_bias)):
                for h in range(FH):
                    sp.dma_start(dst[:].rearrange("p (e h) -> p e h", h=FH)[:, :, h:h + 1],
                                 src[:, h * P:(h + 1) * P].rearrange("e (p o) -> p e o", o=1),
                                 allow_slow_non_contiguous=True).then_inc(loaded, 16)
            sp.wait_ge(loaded, 4 * 16)

        @block.gpsimd
        def _(pool):
            nc.gpsimd.memset(ident[:], 0.0).then_inc(made, 1)
            pool.wait_ge(made, 1)
            nc.gpsimd.affine_select(out=ident[:], in_=ident[:], compare_op=ALU.not_equal,
                                    fill=1.0, base=0, pattern=[[-1, P]],
                                    channel_multiplier=1).then_inc(made, 1)
            pool.wait_ge(made, 2)
            nc.gpsimd.tensor_copy(identb[:], ident[:]).then_inc(made, 1)
            nc.gpsimd.iota(keep["iota_e"][:], [[1, NE]], base=0, channel_multiplier=0,
                           allow_small_or_imprecise_dtypes=True).then_inc(made, 1)
            pool.wait_ge(made, 4)
            nc.gpsimd.tensor_scalar(keep["ebase"][:], keep["iota_e"][:], float(REGION), None,
                                    ALU.mult).then_inc(made, 1)
            nc.gpsimd.memset(keep["ones_row"][:], 1.0).then_inc(made, 1)
            pool.wait_ge(made, 5)
            nc.gpsimd.tensor_copy(keep["base"][:], keep["ebase"][:]).then_inc(made, 1)

        @block.vector
        def _(dve):
            words = [loaded_g, loaded_u, loaded_d]
            W = 4 * CB // 4
            steps = 0

            def step(ins):
                ins.then_inc(link, 1)

            for m in range(3):
                dve.wait_ge(words[m], 16 * LOADS[m])
                w = codes_w[:, m * W:(m + 1) * W]
                lo, hi = (t[:].bitcast(U32)[:, m * W:(m + 1) * W] for t in (lo8, hi8))
                if m:
                    dve.wait_ge(link, steps)
                tmp = [part[:, i, 0:W] for i in range(4)]
                step(nc.vector.tensor_scalar(tmp[0], w, 0x07070707, 2, ALU.bitwise_and,
                                             ALU.logical_shift_left))
                step(nc.vector.tensor_scalar(tmp[1], w, 0x08080808, 4, ALU.bitwise_and,
                                             ALU.logical_shift_left))
                step(nc.vector.tensor_scalar(tmp[2], w, 2, 0x1c1c1c1c, ALU.logical_shift_right,
                                             ALU.bitwise_and))
                step(nc.vector.tensor_scalar(tmp[3], w, 0x80808080, None, ALU.bitwise_and))
                sc = scl32[:, m * 128:(m + 1) * 128]
                step(nc.vector.tensor_copy(sc, scl8[:, m * 128:(m + 1) * 128]))
                dve.wait_ge(link, steps + 4)
                step(nc.vector.tensor_tensor(lo, tmp[0], tmp[1], ALU.bitwise_or))
                step(nc.vector.tensor_tensor(hi, tmp[2], tmp[3], ALU.bitwise_or))
                dve.wait_ge(link, steps + 5)
                step(nc.vector.tensor_scalar(sc, sc, 23, None, ALU.logical_shift_left))
                steps += 8
                dve.wait_ge(link, steps)
                for c in range(4 * m, 4 * m + 4):
                    u = c % 2
                    if c >= 2:
                        dve.wait_ge(turned, c - 1)
                    pair = wq[:, u, :].rearrange("p (b k t) -> p b k t", k=16, t=2)
                    scale = scl32[:, c * 32:(c + 1) * 32].bitcast(F32).rearrange(
                        "p (b o) -> p b o", o=1).to_broadcast([P, 32, 16])
                    for t, src in enumerate((lo8, hi8)):
                        last = nc.vector.tensor_tensor(
                            pair[:, :, :, t],
                            src[:, c * CB:(c + 1) * CB].bitcast(F8).rearrange(
                                "p (b k) -> p b k", k=16), scale, ALU.mult)
                    last.then_inc(quant, 1)
            dve.wait_ge(loaded, 16 * 4)
            nc.vector.tensor_scalar(keep["bu"][:], keep["bu"][:], 1.0, None, ALU.add)

        @block.tensor
        def _(pe):
            pe.wait_ge(made, 3)
            for c in range(CHUNKS):
                u = c % 2
                pe.wait_ge(quant, c + 1)
                if c >= 2:
                    pe.wait_ge(stored, c - 1)
                for t in range(CW // P):
                    last = nc.tensor.transpose(wps[u][:, t * P:(t + 1) * P],
                                               wq[:, u, t * P:(t + 1) * P], identb[:])
                last.then_inc(turned, 1)

        @block.scalar
        def _(act):
            for c in range(CHUNKS):
                act.wait_ge(turned, c + 1)
                nc.scalar.activation(w_all[:, c * CW:(c + 1) * CW], wps[c % 2][:], ACT.Copy,
                                     scale=64.0).then_inc(stored, 1)


def mamba_phase(nc, keep, x, norm_w, norm_b, in_w, conv_w, conv_b, xp_w, dt_w, dt_b, a_log,
                d_par, out_w, rt_w, rt_b, rows_d, x1_d):
    ident, identb = keep["ident"], keep["identb"]
    base, iota_e = keep["base"], keep["iota_e"]
    RING = 4
    AHEAD = 2
    LAG = 3
    with ExitStack() as ctx:
        def sb(name, shape, dt=F32):
            return ctx.enter_context(nc.sbuf_tensor(name, shape, dt))

        def bank(name):
            return ctx.enter_context(nc.psum_tensor(name, [P, 512], F32))

        def sem(name):
            return ctx.enter_context(nc.semaphore(name))

        wx = sb("wx", [P, 2 * DI])
        wc = sb("wc", [P, TAPS, DI])
        xpw = sb("xpw", [P, HALF, P + 2 * NS])
        xpw3 = sb("xpw3", [P, HALF, 3, 2 * NS])
        dtw = sb("dtw", [P, DI])
        ow = sb("ow", [P, HALF, DM])
        a_neg = sb("a_neg", [P, HALF, NS])
        nw, nbias = sb("nw", [P, 1]), sb("nbias", [P, 1])
        cb, dtb, dpar = sb("cb", [P, HALF]), sb("dtb", [P, HALF]), sb("dpar", [P, HALF])
        rtw, rtb = sb("rtw", [P, NE]), sb("rtb", [1, NE])
        sel = sb("sel", [96, 2 * NS, P], BF16)
        tri, onesb = sb("tri", [P, P], BF16), sb("onesb", [P, P], BF16)
        eps_col = sb("eps_col", [P, 1])
        one_col = sb("one_col", [P, 1])
        mv = sb("mv", [P, 2, JT, 2])
        r1 = sb("r1", [P, 2, JT])
        xsr = sb("xsr", [P, 2, 2, HALF, L])
        xs, sres = xsr[:, :, 0], xsr[:, :, 1]
        delta = sb("delta", [P, 2, HALF * L])
        du = sb("du", [P, 2, HALF, L])
        bcs = sb("bcs", [96, 2, L], BF16)
        rows = sb("rows", [P, 2, JT, ROW], BF16)
        slu = sb("slu", [P, 2, JT * TOPK], U32)
        wts = sb("wts", [P, 2, JT, TOPK])
        xa = sb("xa", [P, JT, DM])
        st = sb("st", [P, JT, 6])
        lnv = sb("lnv", [P, JT])
        qv = sb("qv", [P, JT])
        r2 = sb("r2", [P, JT])
        r12 = sb("r12", [P, JT])
        hn = sb("hn", [P, JT, DM])
        hT = sb("hT", [P, L + TAPS - 1])
        lin = sb("lin", [P, 2, HALF, L])
        cw = lin[:].rearrange("p w h l -> p (w h l)")[:, 0:DI * TAPS].rearrange(
            "p (d k) -> p d k", k=TAPS)
        dr = sb("dr", [P, L])
        bcf = sb("bcf", [96, L])
        bcr = sb("bcr", [96, L])
        bcm = sb("bcm", [96, L], BF16)
        zt = sb("zt", [P, HALF * L])
        az = sb("az", [P, HALF * L])
        dA = sb("dA", [P, RING, HALF * L])
        dBu = sb("dBu", [P, 2, HALF * L])
        cs = sb("cs", [P, RING, L])
        hs = sb("hs", [P, RING, HALF * L])
        hc = sb("hc", [P, RING, HALF * L])
        xb = sb("xb", [P, JT, DM])
        y2 = sb("y2", [P, HALF * L])
        o = sb("o", [P, JT, DM])
        st2, mv2, lnv2, rr2 = (sb("st2", [P, JT, 6]), sb("mv2", [P, JT, 2]), sb("lnv2", [P, JT]),
                               sb("rr2", [P, JT]))
        st3, mv3, lnv3, rr3 = (sb("st3", [P, JT, 6]), sb("mv3", [P, JT, 2]), sb("lnv3", [P, JT]),
                               sb("rr3", [P, JT]))
        x1s = sb("x1s", [P, JT, DM])
        xn = sb("xn", [P, JT, DM])
        xnT = sb("xnT", [P, L])
        rest = sb("rest", [P, JT, DM])
        lg = sb("lg", [P, JT, NE])
        top = sb("top", [P, JT, 8])
        topi = sb("topi", [P, JT, 8], U32)
        topf = sb("topf", [P, JT, TOPK])
        hot = sb("hot", [P, JT, TOPK, NE])
        picked = sb("picked", [P, JT, NE], BF16)
        dl, ex = sb("dl", [P, JT, TOPK]), sb("ex", [P, JT, TOPK])
        sm, rc = sb("sm", [P, JT]), sb("rc", [P, JT])
        rk = sb("rk", [P, (JT + 1) * NE])
        pos = sb("pos", [P, JT, NE])
        hp = sb("hp", [P, JT, TOPK, NE])
        slf = sb("slf", [P, JT * TOPK])
        idb = sb("idb", [P, JT], U32)

        pY = [bank("pY0"), bank("pY1")]
        pB = [bank("pB0"), bank("pB1")]
        pC = [bank("pC0"), bank("pC1")]
        pP, pQ = bank("pP"), bank("pQ")

        names = """w_in w_dve w_act w_pool xa_in xb_in x1_ready x1_out
            pre var_ready r1_ready q_ready r2_ready h_ready hT_ps hT_ready xs_ps xs_ready res_ps
            sres_ready silu_ready dr_ps bc_ps dr_ready hi_ready r_ready s_ready dt_ps z_ready
            ln_ready pre_act rs_act sp_pre delta_ready du_ready
            b_ps c_ps da_ready cs_ready dbu_ready h_done hc_ready hc_used
            skip_ready post y_evac y3_ready op_ps o_ready ov_ready or_ready xv_ready xr_ready
            xn_ready xnT_ps xnT_ready rhi_ready rr_ready rmid_ready rows_ready lg_ps lg_done
            m_ready d_ready ex_ready rk_ps rk_done slots_ready post_act sc_done meta
            passed""".split()
        S = {n: sem(n) for n in names}
        block = ctx.enter_context(nc.Block())
        PRE, POST, META = 6, 18, 9
        POST_ACT = 2

        def schedule(eng, batch):
            batch(0, 0)
            batch(1, 1)
            with eng.Fori(1, NB // 2 - 1) as i:
                batch(i * 2, 0)
                batch(i * 2 + 1, 1)
            batch(NB - 2, 0)
            batch(NB - 1, 1)

        def early(b, k):
            return isinstance(b, int) and b < k

        def late(b, k):
            return isinstance(b, int) and b >= NB - k

        def following(b, p, n, k):
            if n + k < NS:
                return b, p, n + k
            return None if late(b, 1) else (b + 1, 1 - p, n + k - NS)

        NW = 16

        @block.sync
        def _(sp):
            def load(dst, src, slow=False):
                sp.dma_start(dst, src, allow_slow_non_contiguous=slow).then_inc(S["w_in"], 16)

            def load_x(b, dst, done):
                sp.dma_start(dst[:], x[bass.ds(b, 1)].rearrange("a (j p) c -> p (a j) c", p=P)
                             ).then_inc(S[done], 16)

            def store_x1(b):
                sp.wait_ge(S["x1_ready"], b + 1)
                sp.dma_start(x1_d[bass.ds(b, 1)].rearrange("a (j p) c -> p (a j) c", p=P), x1s[:]
                             ).then_inc(S["x1_out"], 16)

            load_x(0, xa, "xa_in")
            load(wx[:], in_w)
            load(cw, conv_w.rearrange("(o d) k -> o d k", o=1).to_broadcast([P, DI, TAPS]))
            load(xpw[:], xp_w.rearrange("(h p) n -> p h n", p=P))
            load(dtw[:], dt_w)
            load(ow[:], out_w.rearrange("(h p) n -> p h n", p=P))
            load(a_neg[:], a_log.rearrange("(h p) n -> p h n", p=P))
            load(nw[:], norm_w.rearrange("(p o) -> p o", o=1))
            load(nbias[:], norm_b.rearrange("(p o) -> p o", o=1))
            for dst, src in ((cb, conv_b), (dtb, dt_b), (dpar, d_par)):
                for h in range(HALF):
                    load(dst[:, h:h + 1], src[h * P:(h + 1) * P].rearrange("(p o) -> p o", o=1))
            load(rtw[:].rearrange("p (e o) -> p e o", o=1),
                 rt_w.rearrange("e (p o) -> p e o", o=1), slow=True)
            load(rtb[:], rt_b.rearrange("(o e) -> o e", o=1))
            load_x(0, xb, "xb_in")
            sp.wait_ge(S["h_ready"], 1)
            load_x(1, xa, "xa_in")

            def batch(b, p):
                if not late(b, 2):
                    sp.wait_ge(S["h_ready"], b + 2)
                    load_x(b + 2, xa, "xa_in")
                if not early(b, 1):
                    store_x1(b - 1)
                    load_x(b, xb, "xb_in")

            schedule(sp, batch)
            store_x1(NB - 1)
            sp.wait_ge(S["x1_out"], NB * 16)

        @block.scalar
        def _(act):
            def exp_ln_tables():
                nc.scalar.preload_act_table_set("natural_log_exp_and_others")

            def pre_r1(b, p):
                act.wait_ge(S["var_ready"], b + 1)
                nc.scalar.activation(lnv[:], mv[:, p, :, 1], ACT.Ln, bias=eps_col[:]
                                     ).then_inc(S["rs_act"], 1)
                act.wait_ge(S["rs_act"], 2 * b + 1)
                nc.scalar.activation(r1[:, p], lnv[:], ACT.Exp, scale=-0.5
                                     ).then_inc(S["r1_ready"], 1)

            def pre_r2(b, p):
                act.wait_ge(S["q_ready"], b + 1)
                nc.scalar.activation(lnv[:], qv[:], ACT.Ln, bias=eps_col[:]
                                     ).then_inc(S["rs_act"], 1)
                act.wait_ge(S["rs_act"], 2 * b + 2)
                nc.scalar.activation(r2[:], lnv[:], ACT.Exp, scale=-0.5
                                     ).then_inc(S["r2_ready"], 1)

            def pre_hT(b, p):
                act.wait_ge(S["hT_ps"], b + 1)
                nc.scalar.activation(hT[:, TAPS - 1:], pP[:], ACT.Identity, scale=nw[:],
                                     bias=nbias[:]).then_inc(S["hT_ready"], 1)

            def pre_xs(b, p, h):
                if h == 0 and not early(b, 1):
                    act.wait_ge(S["silu_ready"], b)
                act.wait_ge(S["xs_ps"], 2 * b + h + 1)
                nc.scalar.activation(lin[:, 0, h], pP[:], ACT.Identity,
                                     bias=cb[:, h:h + 1]).then_inc(S["xs_ready"], 1)

            def pre_res(b, p, h):
                act.wait_ge(S["res_ps"], 2 * b + h + 1)
                nc.scalar.activation(lin[:, 1, h], pP[:], ACT.Copy
                                     ).then_inc(S["sres_ready"], 1)

            def pre_silu(b, p):
                act.wait_ge(S["xs_ready"], 2 * b + 2)
                act.wait_ge(S["sres_ready"], 2 * b + 2)
                if not early(b, 2):
                    act.wait_ge(S["y3_ready"], b - 1)
                nc.scalar.activation(xsr[:, p], lin[:], ACT.Silu).then_inc(S["silu_ready"], 1)
                exp_ln_tables()

            def pre_dr(b, p):
                act.wait_ge(S["dr_ps"], b + 1)
                nc.scalar.activation(dr[:], pP[:], ACT.Copy).then_inc(S["dr_ready"], 1)

            def pre_z(b, p, h):
                if h == 0 and not early(b, 1):
                    act.wait_ge(S["delta_ready"], b)
                act.wait_ge(S["dt_ps"], 2 * b + h + 1)
                nc.scalar.activation(zt[:, h * L:(h + 1) * L], pP[:], ACT.Identity,
                                     bias=dtb[:, h:h + 1]).then_inc(S["z_ready"], 1)

            def pre_bc(b, p):
                act.wait_ge(S["bc_ps"], b + 1)
                if not early(b, 1):
                    act.wait_ge(S["r_ready"], b)
                nc.scalar.activation(bcf[:], pP[0:96, :], ACT.Copy)
                nc.scalar.activation(bcs[:, p], pP[0:96, :], ACT.Copy
                                     ).then_inc(S["hi_ready"], 1)

            def pre_softplus(b, p):
                act.wait_ge(S["z_ready"], 2 * b + 2)
                nc.scalar.activation(az[:], zt[:], ACT.Abs).then_inc(S["pre_act"], 1)
                act.wait_ge(S["pre_act"], 2 * b + 1)
                nc.scalar.activation(az[:], az[:], ACT.Exp, scale=-1.0
                                     ).then_inc(S["pre_act"], 1)

            def pre_softplus_ln(b, p):
                act.wait_ge(S["pre_act"], 2 * b + 2)
                nc.scalar.activation(az[:], az[:], ACT.Ln, bias=one_col[:]
                                     ).then_inc(S["ln_ready"], 1)

            def decay(b, p, n):
                g = b * NS + n
                if n == 0:
                    act.wait_ge(S["delta_ready"], b + 1)
                if not early(g, RING):
                    act.wait_ge(S["h_done"], g - RING + 1)
                buf = dA[:, n % RING]
                nc.scalar.activation(buf[:, 0:L], delta[:, p, 0:L], ACT.Exp,
                                     scale=a_neg[:, 0, n:n + 1])
                nc.scalar.activation(buf[:, L + 1:], delta[:, p, L + 1:], ACT.Exp,
                                     scale=a_neg[:, 1, n:n + 1]).then_inc(S["da_ready"], 1)

            def copy_c(b, p, n):
                g = b * NS + n
                act.wait_ge(S["c_ps"], g + 1)
                if not early(g, RING):
                    act.wait_ge(S["hc_ready"], g - RING + 1)
                nc.scalar.activation(cs[:, n % RING], pC[n % 2][:], ACT.Copy
                                     ).then_inc(S["cs_ready"], 1)

            def post_rstd(b, ready, v, l, r, done, k):
                act.wait_ge(ready, b + 1)
                nc.scalar.activation(l[:], v[:, :, 1], ACT.Ln, bias=eps_col[:]
                                     ).then_inc(S["post_act"], 1)
                act.wait_ge(S["post_act"], POST_ACT * b + k)
                nc.scalar.activation(r[:], l[:], ACT.Exp, scale=-0.5).then_inc(done, 1)

            def post_xnT(b, p):
                act.wait_ge(S["xnT_ps"], b + 1)
                nc.scalar.activation(xnT[:], pQ[:], ACT.Copy).then_inc(S["xnT_ready"], 1)

            def post_hi(b, p):
                act.wait_ge(S["xn_ready"], b + 1)
                if not early(b, 1):
                    act.wait_ge(S["meta"], (b - 1) * META + 3)
                nc.scalar.activation(rows[:, p, :, 0:DM], xn[:], ACT.Copy
                                     ).then_inc(S["rhi_ready"], 1)

            def post_lg(b):
                act.wait_ge(S["lg_ps"], b + 1)
                if not early(b, 1):
                    act.wait_ge(S["m_ready"], b)
                nc.scalar.activation(lg[:].rearrange("p j e -> p (j e)"), pQ[:, 0:JT * NE],
                                     ACT.Copy).then_inc(S["lg_done"], 1)

            def post_rank(b):
                act.wait_ge(S["rk_ps"], b + 1)
                if not early(b, 1):
                    act.wait_ge(S["slots_ready"], b)
                nc.scalar.activation(rk[:], pQ[:, 0:(JT + 1) * NE], ACT.Copy
                                     ).then_inc(S["rk_done"], 1)

            def post_mid(b, p):
                act.wait_ge(S["rr_ready"], b + 1)
                nc.scalar.activation(rows[:, p, :, DM:2 * DM], rest[:], ACT.Copy
                                     ).then_inc(S["rmid_ready"], 1)

            def post_exp(b):
                act.wait_ge(S["d_ready"], b + 1)
                nc.scalar.activation(ex[:], dl[:], ACT.Exp).then_inc(S["ex_ready"], 1)

            def pre(b, p, slot):
                if slot == 0:
                    pre_hT(b, p)
                elif slot == 2:
                    pre_xs(b, p, 0)
                elif slot == 5:
                    pre_xs(b, p, 1)
                elif slot == 6:
                    pre_res(b, p, 0)
                    pre_res(b, p, 1)
                elif slot == 7:
                    pre_silu(b, p)
                elif slot == 8:
                    pre_dr(b, p)
                elif slot == 9:
                    pre_bc(b, p)
                elif slot == 10:
                    pre_z(b, p, 0)
                    pre_z(b, p, 1)
                    pre_softplus(b, p)
                elif slot == 11:
                    pre_softplus_ln(b, p)

            def norm(b, p, slot):
                if slot == 9:
                    pre_r1(b, p)
                elif slot == 13:
                    pre_r2(b, p)

            def post(b, p, slot):
                if slot == 6:
                    post_rstd(b, S["ov_ready"], mv2, lnv2, rr2, S["or_ready"], 1)
                elif slot == 8:
                    post_rstd(b, S["xv_ready"], mv3, lnv3, rr3, S["xr_ready"], 2)
                elif slot == 11:
                    post_hi(b, p)
                    post_xnT(b, p)
                elif slot == 12:
                    post_lg(b)
                elif slot == 14:
                    post_exp(b)
                    post_mid(b, p)
                elif slot == 15:
                    post_rank(b)

            def batch(b, p):
                for n in range(NS):
                    ahead = following(b, p, n, AHEAD)
                    if ahead:
                        decay(*ahead)
                    after = following(b, p, n, 1)
                    if after:
                        copy_c(*after)
                    if not early(b, 1):
                        post(b - 1, 1 - p, n)
                    if not late(b, 1):
                        pre(b + 1, 1 - p, n)
                    if not late(b, 2):
                        norm(b + 2, p, n)

            exp_ln_tables()
            act.wait_ge(S["w_in"], NW * 16)
            nc.scalar.activation(a_neg[:], a_neg[:], ACT.Exp).then_inc(S["w_act"], 1)
            act.wait_ge(S["w_pool"], 12)
            act.wait_ge(S["w_dve"], 7)
            for b in range(2):
                pre_r1(b, b)
                pre_r2(b, b)
            for slot in range(NS):
                pre(0, 0, slot)
            for n in range(AHEAD):
                decay(0, 0, n)
            copy_c(0, 0, 0)
            schedule(act, batch)
            for slot in range(NS):
                post(NB - 1, 1, slot)

        @block.gpsimd
        def _(pool):
            def scaled_state(b, n):
                g = b * NS + n
                pool.wait_ge(S["h_done"], g + 1)
                pool.wait_ge(S["cs_ready"], g + 1)
                if not early(g, RING):
                    pool.wait_ge(S["hc_used"], g - RING + 1)
                nc.gpsimd.tensor_tensor(
                    hc[:, n % RING].rearrange("p (h l) -> p h l", h=HALF),
                    hs[:, n % RING].rearrange("p (h l) -> p h l", h=HALF),
                    cs[:, n % RING].rearrange("p (o l) -> p o l", o=1).to_broadcast([P, HALF, L]),
                    ALU.mult).then_inc(S["hc_ready"], 1)

            def scatter(b, p, k, j):
                words = rows[:].bitcast(U32)[:, p]
                if j == 0:
                    if k == 0:
                        pool.wait_ge(S["rows_ready"], b + 1)
                        pool.wait_ge(S["slots_ready"], b + 1)
                        if not early(b, 1):
                            pool.wait_ge(S["meta"], b * META)
                        pool.sem_inc(S["passed"], 1)
                        nc.gpsimd.tensor_copy(words[:, :, ID], idb[:]).then_inc(S["meta"], 1)
                    else:
                        pool.wait_ge(S["sc_done"], b * 256 + 64 * k)
                        pool.sem_inc(S["passed"], 1)
                        nc.gpsimd.tensor_scalar(words[:, :, ID], words[:, :, ID], 1, None,
                                                ALU.add).then_inc(S["meta"], 1)
                    nc.gpsimd.tensor_copy(words[:, :, WEIGHT].bitcast(F32), wts[:, p, :, k]
                                          ).then_inc(S["meta"], 1)
                    pool.wait_ge(S["meta"], b * META + 2 * k + 2)
                    pool.sem_inc(S["passed"], 1)
                    if k == TOPK - 1:
                        nc.gpsimd.tensor_scalar(idb[:], idb[:], TOPK * L, None, ALU.add
                                                ).then_inc(S["meta"], 1)
                c = j * TOPK + k
                nc.gpsimd.indirect_dma_start(
                    rows_d, bass.IndirectOffsetOnAxis(ap=slu[:, p, c:c + 1], axis=0),
                    words[:, j, :], None).then_inc(S["sc_done"], 16)

            def batch(b, p):
                for n in range(NS):
                    scaled_state(b, n)
                    if not early(b, 2):
                        scatter(b - 2, p, n // JT, n % JT)

            nc.gpsimd.memset(sel[:], 0.0).then_inc(S["w_pool"], 1)
            nc.gpsimd.memset(tri[:], 0.0).then_inc(S["w_pool"], 1)
            nc.gpsimd.memset(onesb[:], 1.0).then_inc(S["w_pool"], 1)
            nc.gpsimd.memset(hT[:, 0:TAPS - 1], 0.0).then_inc(S["w_pool"], 1)
            nc.gpsimd.memset(eps_col[:], EPS).then_inc(S["w_pool"], 1)
            nc.gpsimd.memset(one_col[:], 1.0).then_inc(S["w_pool"], 1)
            nc.gpsimd.memset(dA[:, :, L:L + 1], 0.0).then_inc(S["w_pool"], 1)
            nc.gpsimd.iota(idb[:], [[TOPK * P, JT]], base=0, channel_multiplier=TOPK
                           ).then_inc(S["w_pool"], 1)
            for part in range(3):
                pool.wait_ge(S["w_pool"], 8 + part)
                nc.gpsimd.affine_select(out=sel[:], in_=sel[:], compare_op=ALU.not_equal,
                                        fill=1.0, base=-32 * part, pattern=[[-1, 2 * NS], [0, P]],
                                        channel_multiplier=1).then_inc(S["w_pool"], 1)
            nc.gpsimd.affine_select(out=tri[:], in_=tri[:], compare_op=ALU.is_ge, fill=1.0,
                                    base=0, pattern=[[-1, P]], channel_multiplier=1
                                    ).then_inc(S["w_pool"], 1)
            pool.wait_ge(S["w_pool"], 12)
            schedule(pool, batch)
            for b in range(NB - 2, NB):
                for i in range(JT * TOPK):
                    scatter(b, b % 2, i // JT, i % JT)
            pool.wait_ge(S["sc_done"], NB * 256)

        @block.vector
        def _(dve):
            def stats(src, sts, chain, at):
                for j in range(JT):
                    nc.vector.bn_stats(sts[:, j, :], src[:, j, :]).then_inc(chain, 1)
                dve.wait_ge(chain, at + JT)
                dve.sem_inc(S["passed"], 1)

            def aggregate(m, sts, done):
                for j in range(JT):
                    last = nc.vector.bn_aggr(m[:, j, :], sts[:, j, :])
                last.then_inc(done, 1)

            def normal(dst, src, m, r, last_sem):
                for j in range(JT):
                    last = nc.vector.tensor_scalar(dst[:, j, :], src[:, j, :], m[:, j, 0:1],
                                                   r[:, j:j + 1], ALU.subtract, ALU.mult)
                last.then_inc(last_sem, 1)

            def pre_stats(b, p):
                dve.wait_ge(S["xa_in"], b * 16 + 16)
                if not early(b, 2):
                    dve.wait_ge(S["skip_ready"], b - 1)
                stats(xa, st, S["pre"], b * PRE)
                aggregate(mv[:, p], st, S["var_ready"])

            def pre_q(b, p):
                dve.wait_ge(S["r1_ready"], b + 1)
                nc.vector.tensor_tensor(qv[:], mv[:, p, :, 1], r1[:, p], ALU.mult
                                        ).then_inc(S["pre"], 1)
                dve.wait_ge(S["pre"], b * PRE + 5)
                nc.vector.tensor_tensor(qv[:], qv[:], r1[:, p], ALU.mult
                                        ).then_inc(S["q_ready"], 1)

            def pre_norm(b, p):
                dve.wait_ge(S["r2_ready"], b + 1)
                nc.vector.tensor_tensor(r12[:], r1[:, p], r2[:], ALU.mult
                                        ).then_inc(S["pre"], 1)
                dve.wait_ge(S["pre"], b * PRE + 6)
                if not early(b, 1):
                    dve.wait_ge(S["hT_ps"], b)
                normal(hn, xa, mv[:, p], r12, S["h_ready"])

            def pre_split(b, p):
                dve.wait_ge(S["hi_ready"], b + 1)
                nc.vector.tensor_tensor(bcr[:], bcf[:], bcs[:, p], ALU.subtract
                                        ).then_inc(S["r_ready"], 1)
                dve.wait_ge(S["r_ready"], b + 1)
                nc.vector.tensor_copy(bcs[32:64, p], bcr[32:64, :]).then_inc(S["sp_pre"], 1)
                nc.vector.tensor_copy(bcm[64:96, :], bcr[64:96, :]).then_inc(S["sp_pre"], 1)
                dve.wait_ge(S["sp_pre"], b * 2 + 2)
                nc.vector.tensor_tensor(bcs[64:96, p], bcr[64:96, :], bcm[64:96, :],
                                        ALU.subtract).then_inc(S["s_ready"], 1)

            def pre_delta(b, p):
                dve.wait_ge(S["ln_ready"], b + 1)
                nc.vector.scalar_tensor_tensor(delta[:, p], zt[:], 0.0, az[:], ALU.max, ALU.add
                                               ).then_inc(S["delta_ready"], 1)
                dve.wait_ge(S["delta_ready"], b + 1)
                nc.vector.tensor_tensor(du[:, p].rearrange("p h l -> p (h l)"), delta[:, p],
                                        xs[:, p].rearrange("p h l -> p (h l)"), ALU.mult
                                        ).then_inc(S["du_ready"], 1)

            def drive(b, p, n):
                g = b * NS + n
                if n == 0:
                    dve.wait_ge(S["du_ready"], b + 1)
                dve.wait_ge(S["b_ps"], g + 1)
                if not early(g, 2):
                    dve.wait_ge(S["h_done"], g - 1)
                nc.vector.tensor_tensor(
                    dBu[:, n % 2].rearrange("p (h l) -> p h l", h=HALF), du[:, p],
                    pB[n % 2][:].rearrange("p (o l) -> p o l", o=1).to_broadcast([P, HALF, L]),
                    ALU.mult).then_inc(S["dbu_ready"], 1)

            def scan(b, n):
                g = b * NS + n
                dve.wait_ge(S["dbu_ready"], g + 1)
                dve.wait_ge(S["da_ready"], g + 1)
                if not early(g, RING):
                    dve.wait_ge(S["hc_ready"], g - RING + 1)
                nc.vector.tensor_tensor_scan(hs[:, n % RING], dA[:, n % RING], dBu[:, n % 2],
                                             0.0, ALU.mult, ALU.add).then_inc(S["h_done"], 1)

            def skip(b, p):
                dve.wait_ge(S["xb_in"], b * 16 + 16)
                if not early(b, 1):
                    dve.wait_ge(S["x1_ready"], b)
                normal(o, xb, mv[:, p], r1[:, p], S["skip_ready"])

            def post_y(b, p):
                dve.wait_ge(S["hc_used"], (b + 1) * NS)
                if not early(b, 1):
                    dve.wait_ge(S["op_ps"], b)
                for h in range(HALF):
                    last = nc.vector.scalar_tensor_tensor(
                        y2[:, h * L:(h + 1) * L], xs[:, p, h], dpar[:, h:h + 1], pY[h][:],
                        ALU.mult, ALU.add)
                last.then_inc(S["y_evac"], 1)
                dve.wait_ge(S["y_evac"], b + 1)
                nc.vector.tensor_tensor(y2[:], y2[:], sres[:, p].rearrange("p h l -> p (h l)"),
                                        ALU.mult).then_inc(S["y3_ready"], 1)

            def post_o(b):
                dve.wait_ge(S["skip_ready"], b + 1)
                dve.wait_ge(S["op_ps"], b + 1)
                nc.vector.tensor_tensor(o[:].rearrange("p j c -> p (j c)"),
                                        o[:].rearrange("p j c -> p (j c)"), pQ[:], ALU.add
                                        ).then_inc(S["o_ready"], 1)
                dve.wait_ge(S["o_ready"], b + 1)
                stats(o, st2, S["post"], b * POST)
                aggregate(mv2, st2, S["ov_ready"])

            def post_x1(b):
                dve.wait_ge(S["or_ready"], b + 1)
                normal(o, o, mv2, rr2, S["post"])
                dve.wait_ge(S["post"], b * POST + 5)
                if not early(b, 1):
                    dve.wait_ge(S["x1_out"], b * 16)
                nc.vector.tensor_tensor(x1s[:], o[:], xb[:], ALU.add
                                        ).then_inc(S["x1_ready"], 1)
                dve.wait_ge(S["x1_ready"], b + 1)
                stats(x1s, st3, S["post"], b * POST + 5)
                aggregate(mv3, st3, S["xv_ready"])

            def post_xn(b):
                dve.wait_ge(S["xr_ready"], b + 1)
                normal(xn, x1s, mv3, rr3, S["xn_ready"])

            def post_rest(b, p):
                dve.wait_ge(S["rhi_ready"], b + 1)
                nc.vector.tensor_tensor(rest[:], xn[:], rows[:, p, :, 0:DM], ALU.subtract
                                        ).then_inc(S["rr_ready"], 1)

            def post_lo(b, p):
                dve.wait_ge(S["rmid_ready"], b + 1)
                nc.vector.tensor_tensor(rows[:, p, :, 2 * DM:3 * DM], rest[:],
                                        rows[:, p, :, DM:2 * DM], ALU.subtract
                                        ).then_inc(S["rows_ready"], 1)

            def post_top(b):
                dve.wait_ge(S["lg_done"], b + 1)
                dve.sem_inc(S["passed"], 1)
                for j in range(JT):
                    last = nc.vector.max(top[:, j], lg[:, j])
                last.then_inc(S["post"], 1)
                dve.wait_ge(S["post"], b * POST + 10)
                dve.sem_inc(S["passed"], 1)
                for j in range(JT):
                    last = nc.vector.max_index(topi[:, j], top[:, j], lg[:, j])
                last.then_inc(S["post"], 1)
                nc.vector.tensor_tensor(dl[:], top[:, :, 0:TOPK],
                                        top[:, :, 0:1].to_broadcast([P, JT, TOPK]), ALU.subtract
                                        ).then_inc(S["d_ready"], 1)
                dve.wait_ge(S["post"], b * POST + 11)
                nc.vector.tensor_copy(topf[:], topi[:, :, 0:TOPK]).then_inc(S["post"], 1)
                dve.wait_ge(S["post"], b * POST + 12)
                hotf = hot[:].rearrange("p j k e -> p (j k) e")
                nc.vector.tensor_tensor(
                    hotf, iota_e[:].rearrange("p (o e) -> p o e", o=1).to_broadcast(
                        [P, JT * TOPK, NE]),
                    topf[:].rearrange("p j (k o) -> p (j k) o", o=1).to_broadcast(
                        [P, JT * TOPK, NE]), ALU.is_equal).then_inc(S["post"], 1)
                dve.wait_ge(S["post"], b * POST + 13)
                with nc.allow_low_precision(reason="sums of at most one 1: exact in bf16"):
                    for j in range(JT):
                        last = nc.vector.tensor_reduce(picked[:, j],
                                                       hot[:, j].rearrange("p k e -> p e k"),
                                                       AX.X, ALU.add)
                last.then_inc(S["m_ready"], 1)

            def post_slots(b, p):
                dve.wait_ge(S["ex_ready"], b + 1)
                nc.vector.tensor_reduce(sm[:], ex[:], AX.X, ALU.add).then_inc(S["post"], 1)
                dve.wait_ge(S["post"], b * POST + 14)
                nc.vector.reciprocal(rc[:], sm[:]).then_inc(S["post"], 1)
                dve.wait_ge(S["post"], b * POST + 15)
                if not early(b, 1):
                    dve.wait_ge(S["meta"], (b - 1) * META + 3)
                nc.vector.tensor_tensor(
                    wts[:, p], ex[:],
                    rc[:].rearrange("p (j o) -> p j o", o=1).to_broadcast([P, JT, TOPK]),
                    ALU.mult)
                dve.wait_ge(S["rk_done"], b + 1)
                nc.vector.tensor_tensor(
                    pos[:], rk[:, 0:JT * NE].rearrange("p (j e) -> p j e", e=NE),
                    base[:].rearrange("p (o e) -> p o e", o=1).to_broadcast([P, JT, NE]),
                    ALU.add).then_inc(S["post"], 1)
                dve.wait_ge(S["post"], b * POST + 16)
                nc.vector.tensor_tensor(base[:], base[:], rk[:, JT * NE:], ALU.add)
                for j in range(JT):
                    last = nc.vector.tensor_tensor(
                        hp[:, j], hot[:, j],
                        pos[:, j:j + 1].to_broadcast([P, TOPK, NE]), ALU.mult)
                last.then_inc(S["post"], 1)
                dve.wait_ge(S["post"], b * POST + 17)
                nc.vector.tensor_reduce(slf[:], hp[:].rearrange("p j k e -> p (j k) e"), AX.X,
                                        ALU.add).then_inc(S["post"], 1)
                dve.wait_ge(S["post"], b * POST + 18)
                nc.vector.tensor_copy(slu[:, p], slf[:]).then_inc(S["slots_ready"], 1)

            def pre(b, p, slot):
                if slot == 11:
                    pre_split(b, p)
                elif slot == 13:
                    pre_delta(b, p)

            def norm(b, p, slot):
                if slot == 8:
                    pre_stats(b, p)
                elif slot == 12:
                    pre_q(b, p)
                elif slot == 14:
                    pre_norm(b, p)

            def post(b, p, slot):
                if slot == 2:
                    post_y(b, p)
                elif slot == 5:
                    post_o(b)
                elif slot == 7:
                    post_x1(b)
                elif slot == 9:
                    post_xn(b)
                elif slot == 13:
                    post_top(b)
                    post_rest(b, p)
                elif slot == 15:
                    post_lo(b, p)
                    post_slots(b, p)

            def batch(b, p):
                for n in range(NS):
                    after = following(b, p, n, 1)
                    if after:
                        drive(*after)
                    scan(b, n)
                    if n == 8:
                        skip(b, p)
                    if not early(b, 1):
                        post(b - 1, 1 - p, n)
                    if not late(b, 1):
                        pre(b + 1, 1 - p, n)
                    if not late(b, 2):
                        norm(b + 2, p, n)

            dve.wait_ge(S["w_in"], NW * 16)
            dve.wait_ge(S["w_act"], 1)
            nc.vector.tensor_scalar(a_neg[:], a_neg[:], -1.0, None, ALU.mult
                                    ).then_inc(S["w_dve"], 1)
            for k in range(TAPS):
                nc.vector.tensor_tensor(wc[:, k], wx[:, 0:DI], cw[:, :, k], ALU.mult
                                        ).then_inc(S["w_dve"], 1)
            for h in range(HALF):
                nc.vector.tensor_copy(
                    xpw3[:, h], xpw[:, h:h + 1, P:].to_broadcast([P, 3, 2 * NS])
                    ).then_inc(S["w_dve"], 1)
            dve.wait_ge(S["w_pool"], 12)
            for b in range(2):
                for slot in range(NS):
                    norm(b, b, slot)
            for slot in range(NS):
                pre(0, 0, slot)
            drive(0, 0, 0)
            schedule(dve, batch)
            for slot in range(NS):
                post(NB - 1, 1, slot)

        @block.tensor
        def _(pe):
            mm = nc.tensor.matmul

            def pre_hT(b, p):
                pe.wait_ge(S["h_ready"], b + 1)
                if not early(b, 1):
                    pe.wait_ge(S["z_ready"], 2 * b)
                for j in range(JT):
                    last = nc.tensor.transpose(pP[:, j * P:(j + 1) * P], hn[:, j, :], ident[:])
                last.then_inc(S["hT_ps"], 1)

            def pre_in(b, p, h, taps):
                if taps[0] == 0:
                    if h == 0:
                        pe.wait_ge(S["hT_ready"], b + 1)
                    else:
                        pe.wait_ge(S["xs_ready"], 2 * b + 1)
                for k in taps:
                    last = mm(pP[:], wc[:, k, h * P:(h + 1) * P], hT[:, k:k + L],
                              start=(k == 0), stop=(k == TAPS - 1))
                if taps[-1] == TAPS - 1:
                    last.then_inc(S["xs_ps"], 1)

            def pre_res(b, p, h):
                if h == 0:
                    pe.wait_ge(S["xs_ready"], 2 * b + 2)
                else:
                    pe.wait_ge(S["sres_ready"], 2 * b + 1)
                mm(pP[:], wx[:, DI + h * P:DI + (h + 1) * P], hT[:, TAPS - 1:], start=True,
                   stop=True).then_inc(S["res_ps"], 1)

            def pre_dr(b, p):
                pe.wait_ge(S["silu_ready"], b + 1)
                for h in range(HALF):
                    last = mm(pP[:], xpw[:, h, 0:P], xs[:, p, h], start=(h == 0),
                              stop=(h == HALF - 1))
                last.then_inc(S["dr_ps"], 1)

            def pre_dt(b, p, h):
                if h == 0:
                    pe.wait_ge(S["dr_ready"], b + 1)
                    pe.wait_ge(S["hi_ready"], b + 1)
                else:
                    pe.wait_ge(S["z_ready"], 2 * b + 1)
                mm(pP[:], dtw[:, h * P:(h + 1) * P], dr[:], start=True, stop=True
                   ).then_inc(S["dt_ps"], 1)

            def pre_bc(b, p):
                pe.wait_ge(S["dr_ready"], b + 1)
                for h in range(HALF):
                    last = mm(pP[0:96, :], xpw3[:, h].rearrange("p t n -> p (t n)"),
                              xs[:, p, h], start=(h == 0), stop=(h == HALF - 1))
                last.then_inc(S["bc_ps"], 1)

            def spread_b(b, p, n):
                g = b * NS + n
                if n == 0:
                    pe.wait_ge(S["s_ready"], b + 1)
                if not early(g, 2):
                    pe.wait_ge(S["dbu_ready"], g - 1)
                mm(pB[n % 2][:], sel[:, n, :], bcs[:, p], start=True, stop=True
                   ).then_inc(S["b_ps"], 1)

            def spread_c(b, p, n):
                g = b * NS + n
                if not early(g, 2):
                    pe.wait_ge(S["cs_ready"], g - 1)
                mm(pC[n % 2][:], sel[:, NS + n, :], bcs[:, p], start=True, stop=True
                   ).then_inc(S["c_ps"], 1)

            def gather_state(b, n, h):
                g = b * NS + n
                if h == 0:
                    pe.wait_ge(S["hc_ready"], g + 1)
                    if n == 0 and not early(b, 1):
                        pe.wait_ge(S["y_evac"], b)
                last = mm(pY[h][:], ident[:], hc[:, n % RING, h * L:(h + 1) * L],
                          start=(n == 0), stop=(n == NS - 1))
                if h == HALF - 1:
                    last.then_inc(S["hc_used"], 1)

            def post_out(b):
                pe.wait_ge(S["y3_ready"], b + 1)
                if not early(b, 1):
                    pe.wait_ge(S["rk_done"], b)
                for j in range(JT):
                    for h in range(HALF):
                        last = mm(pQ[:, j * DM:(j + 1) * DM],
                                  y2[:, h * L + j * P:h * L + (j + 1) * P], ow[:, h],
                                  start=(h == 0), stop=(h == HALF - 1))
                last.then_inc(S["op_ps"], 1)

            def post_xnT(b):
                pe.wait_ge(S["xn_ready"], b + 1)
                pe.wait_ge(S["o_ready"], b + 1)
                for j in range(JT):
                    last = nc.tensor.transpose(pQ[:, j * P:(j + 1) * P], xn[:, j, :], ident[:])
                last.then_inc(S["xnT_ps"], 1)

            def post_logits(b):
                pe.wait_ge(S["xnT_ready"], b + 1)
                for j in range(JT):
                    mm(pQ[:, j * NE:(j + 1) * NE], xnT[:, j * P:(j + 1) * P], rtw[:],
                       start=True, stop=False)
                    last = mm(pQ[:, j * NE:(j + 1) * NE], keep["ones_row"][:], rtb[:],
                              start=False, stop=True)
                last.then_inc(S["lg_ps"], 1)

            def post_rank(b):
                pe.wait_ge(S["m_ready"], b + 1)
                pe.wait_ge(S["lg_done"], b + 1)
                for j in range(JT):
                    for i in range(j + 1):
                        mm(pQ[:, j * NE:(j + 1) * NE], (tri if i == j else onesb)[:],
                           picked[:, i], start=(i == 0), stop=(i == j))
                for i in range(JT):
                    last = mm(pQ[:, JT * NE:(JT + 1) * NE], onesb[:], picked[:, i],
                              start=(i == 0), stop=(i == JT - 1))
                last.then_inc(S["rk_ps"], 1)

            def first_of(b, p, slot, pre, post):
                if pre and slot == 0:
                    pre_hT(b + 1, 1 - p)
                elif pre and slot == 1:
                    pre_in(b + 1, 1 - p, 0, (0, 1))
                elif pre and slot == 2:
                    pre_in(b + 1, 1 - p, 0, (2, 3))
                elif pre and slot == 3:
                    pre_in(b + 1, 1 - p, 1, (0, 1))
                elif post and slot == 4:
                    post_out(b - 1)
                elif pre and slot == 5:
                    pre_in(b + 1, 1 - p, 1, (2, 3))
                elif pre and slot == 6:
                    pre_res(b + 1, 1 - p, 0)
                elif pre and slot == 9:
                    pre_bc(b + 1, 1 - p)
                elif pre and slot == 10:
                    pre_dt(b + 1, 1 - p, 0)
                elif post and slot == 12:
                    post_logits(b - 1)

            def second_of(b, p, slot, pre, post):
                if pre and slot == 6:
                    pre_res(b + 1, 1 - p, 1)
                elif pre and slot == 8:
                    pre_dr(b + 1, 1 - p)
                elif pre and slot == 10:
                    pre_dt(b + 1, 1 - p, 1)
                elif post and slot == 11:
                    post_xnT(b - 1)
                elif post and slot == 14:
                    post_rank(b - 1)

            def batch(b, p):
                pre, post = not late(b, 1), not early(b, 1)
                for n in range(NS):
                    second = following(b, p, n, 2)
                    if second:
                        spread_b(*second)
                    if n >= LAG:
                        first_of(b, p, n, pre, post)
                    before = (b, n - LAG) if n >= LAG else (b - 1, NS + n - LAG)
                    if n >= LAG or post:
                        gather_state(*before, 0)
                    if second:
                        spread_c(*second)
                    if n >= LAG or post:
                        gather_state(*before, 1)
                    if n < LAG:
                        first_of(b, p, n, pre, post)
                    second_of(b, p, n, pre, post)

            pe.wait_ge(S["w_dve"], 7)
            pe.wait_ge(S["w_pool"], 12)
            for slot in range(NS):
                first_of(-1, 1, slot, True, False)
                second_of(-1, 1, slot, True, False)
            spread_b(0, 0, 0)
            spread_b(0, 0, 1)
            spread_c(0, 0, 0)
            spread_c(0, 0, 1)
            schedule(pe, batch)
            for n in range(NS - LAG, NS):
                for h in range(HALF):
                    gather_state(NB - 1, n, h)
            for slot in range(NS):
                first_of(NB, 0, slot, False, True)
                second_of(NB, 0, slot, False, True)


def expert_phase(nc, keep, d_bias, rows_d, yk_d):
    identb, w_all = keep["identb"], keep["w_all"]
    RING = 8
    LEAD, LAG = 2, 2
    with ExitStack() as ctx:
        def sb(name, shape, dt=F32):
            return ctx.enter_context(nc.sbuf_tensor(name, shape, dt))

        def bank(name, dt=F32):
            return ctx.enter_context(nc.psum_tensor(name, [P, 2048 // (4 if dt == F32 else 2)],
                                                    dt))

        def sem(name):
            return ctx.enter_context(nc.semaphore(name))

        cnt = sb("cnt", [1, NE])
        cnti = sb("cnti", [1, NE], I32)
        ntile = sb("ntile", [1, NE])
        cum = sb("cum", [1, NE])
        ones_e = sb("ones_e", [1, NE])
        first = sb("first", [1, NE])
        ti = sb("ti", [1, NT])
        cmp = sb("cmp", [1, NT, NE])
        ef = sb("ef", [1, NT])
        valid = sb("valid", [1, NT])
        rowf = sb("rowf", [1, NT])
        tab_e = sb("tab_e", [1, NT], I32)
        tab_r = sb("tab_r", [1, NT], I32)
        endi = sb("endi", [1, NE], I32)
        pad = sb("pad", [P, 2, ROW], BF16)
        xr = sb("xr", [P, RING, 2, ROW], BF16)
        xT = sb("xT", [P, 4, 3 * TILE], BF16)
        gt = sb("gt", [P, 2, FH * TILE])
        sg = sb("sg", [P, 2, FH * TILE])
        ut = sb("ut", [P, 2, FH * TILE])
        it = sb("it", [P, 2, FH * TILE])
        yo = sb("yo", [P, 4, 2, DM])
        bdf, bdr = sb("bdf", [96, NE * DM]), sb("bdr", [96, NE * DM])
        bds, bdm = sb("bds", [96, NE * DM], BF16), sb("bdm", [96, NE * DM], BF16)
        pick = sb("pick", [96, P], BF16)
        wd32 = sb("wd32", [P, NE * FH * DM])
        pX = [bank(f"pX{i}", BF16) for i in range(2)]
        pG = [bank(f"pG{i}") for i in range(2)]
        pU = [bank(f"pU{i}") for i in range(2)]
        pO = [bank(f"pO{i}") for i in range(2)]
        wd_ready, bd_in, bdh_ready, bd_link, bd_ready, pick_made = (
            sem(n) for n in ("wd_ready", "bd_in", "bdh_ready", "bd_link", "bd_ready",
                             "pick_made"))
        padded, pad_made, t_link, table_ready, xT_ps, xT_ready, g_ps, u_ps = (
            sem(n) for n in ("padded", "pad_made", "t_link", "table_ready", "xT_ps", "xT_ready",
                             "g_ps", "u_ps"))
        g_ready, u_ready, sg_ready, glu_ready, it_ready, o_ps, y_ready, e_passed = (
            sem(n) for n in ("g_ready", "u_ready", "sg_ready", "glu_ready", "it_ready", "o_ps",
                             "y_ready", "e_passed"))
        rows_in = [sem(f"rows_in{r}") for r in range(RING)]
        y_out = [sem(f"y_out{q}") for q in range(4)]
        block = ctx.enter_context(nc.Block())

        def schedule(eng, tile):
            for t in range(RING):
                tile(t, t)
            with eng.Fori(1, NT // RING - 1) as i:
                for u in range(RING):
                    tile(i * RING + u, u)
            for t in range(NT - RING, NT):
                tile(t, t % RING)

        def early(t, k):
            return isinstance(t, int) and t < k

        def late(t, k):
            return isinstance(t, int) and t >= NT - k

        def scattered(t, u):
            if isinstance(t, int):
                return 32 * (t // 4 + 1)
            return (t - u) * 8 + (u // 4) * 32 + 32

        @block.sync
        def _(sp):
            def tile(t, u):
                row = sp.value_load(tab_r[0:1, bass.ds(t, 1)], min_val=0, max_val=NE * REGION)
                if not early(t, RING):
                    sp.wait_ge(y_out[u % 4], scattered(t - RING, u))
                sp.dma_start(xr[:].bitcast(U32)[:, u], rows_d[bass.ds(row, TILE), :].rearrange(
                    "(p s) c -> p s c", s=2)).then_inc(rows_in[u], 16)

            sp.dma_start(bdf[:], d_bias.rearrange("(o e) h -> o (e h)", o=1).to_broadcast(
                [96, NE * DM])).then_inc(bd_in, 16)
            sp.wait_ge(pad_made, 2)
            sp.wait_ge(table_ready, 1)
            with sp.Fori(0, NE) as e:
                end = sp.value_load(endi[0:1, bass.ds(e, 1)], min_val=0,
                                    max_val=NE * REGION - TILE)
                sp.dma_start(rows_d[bass.ds(end, TILE), :].rearrange("(p s) c -> p s c", s=2),
                             pad[:].bitcast(U32)).then_inc(padded, 16)
            sp.dma_start(rows_d[NE * REGION:NE * REGION + TILE, :].rearrange(
                "(p s) c -> p s c", s=2), pad[:].bitcast(U32)).then_inc(padded, 16)
            sp.wait_ge(padded, (NE + 1) * 16)
            sp.wait_ge(table_ready, 2)
            schedule(sp, tile)

        @block.gpsimd
        def _(pool):
            nc.gpsimd.memset(pad[:], 0.0).then_inc(pad_made, 1)
            pool.wait_ge(pad_made, 1)
            nc.gpsimd.iota(pad[:].bitcast(U32)[:, :, ID], [[0, 2]], base=NO_TOKEN,
                           channel_multiplier=0).then_inc(pad_made, 1)
            nc.gpsimd.iota(ti[:], [[1, NT]], base=0, channel_multiplier=0,
                           allow_small_or_imprecise_dtypes=True).then_inc(pad_made, 1)
            nc.gpsimd.memset(ones_e[:], 1.0).then_inc(pad_made, 1)
            nc.gpsimd.memset(pick[:], 0.0).then_inc(pick_made, 1)
            for part in range(3):
                pool.wait_ge(pick_made, part + 1)
                nc.gpsimd.affine_select(out=pick[:], in_=pick[:], compare_op=ALU.not_equal,
                                        fill=1.0, base=-32 * part, pattern=[[0, P]],
                                        channel_multiplier=1).then_inc(pick_made, 1)

            def tile(t, u):
                pool.wait_ge(y_ready, t + 1)
                pool.sem_inc(e_passed, 1)
                ids = xr[:].bitcast(U32)
                for sx in range(2):
                    nc.gpsimd.indirect_dma_start(
                        yk_d, bass.IndirectOffsetOnAxis(ap=ids[:, u, sx, ID:ID + 1],
                                                        axis=0),
                        yo[:, u % 4, sx, :], None, bounds_check=TOKENS * TOPK - 1,
                        oob_is_err=False).then_inc(y_out[u % 4], 16)

            schedule(pool, tile)
            for q in range(4):
                pool.wait_ge(y_out[q], 8 * NT)

        @block.scalar
        def _(act):
            def evac_x(t, u):
                act.wait_ge(xT_ps, t + 1)
                if not early(t, 4):
                    act.wait_ge(u_ps, t - 3)
                nc.scalar.activation(xT[:, u % 4], pX[u % 2][:, 0:3 * TILE], ACT.Copy
                                     ).then_inc(xT_ready, 1)

            def evac_y(t, u):
                act.wait_ge(o_ps, t + 1)
                if not early(t, 4):
                    act.wait_ge(y_out[u % 4], scattered(t - 4, (u - 4) % RING))
                weight = xr[:].bitcast(F32)[:, u, :, WEIGHT]
                for sx in range(2):
                    last = nc.scalar.activation(yo[:, u % 4, sx],
                                                pO[u % 2][:, sx * DM:(sx + 1) * DM],
                                                ACT.Copy, scale=weight[:, sx:sx + 1])
                last.then_inc(y_ready, 1)

            def tile(t, u):
                q = u % 2
                if not early(t, LAG):
                    evac_y(t - LAG, (u - LAG) % RING)
                act.wait_ge(g_ready, t + 1)
                if not early(t, 2):
                    act.wait_ge(glu_ready, t - 1)
                nc.scalar.activation(sg[:, q], gt[:, q], ACT.Sigmoid, scale=SIG_SCALE
                                     ).then_inc(sg_ready, 1)
                if not late(t, LEAD):
                    evac_x(t + LEAD, (u + LEAD) % RING)

            nc.scalar.activation(wd32[:], w_all[:, 8 * CW:], ACT.Copy).then_inc(wd_ready, 1)
            act.wait_ge(bd_in, 16)
            nc.scalar.activation(bds[:], bdf[:], ACT.Copy).then_inc(bdh_ready, 1)
            for t in range(LEAD):
                evac_x(t, t)
            schedule(act, tile)
            for t in range(NT - LAG, NT):
                evac_y(t, t % RING)

        @block.vector
        def _(dve):
            dve.wait_ge(pad_made, 4)
            nc.vector.tensor_copy(endi[:], keep["base"][0:1, :]).then_inc(table_ready, 1)
            link = [0]

            def chain(ins):
                link[0] += 1
                ins.then_inc(t_link, 1)
                dve.wait_ge(t_link, link[0])

            chain(nc.vector.tensor_tensor(cnt[:], keep["base"][0:1, :], keep["ebase"][0:1, :],
                                          ALU.subtract))
            chain(nc.vector.tensor_scalar(cnti[:], cnt[:], float(TILE - 1), None, ALU.add))
            chain(nc.vector.tensor_scalar(cnti[:], cnti[:], 8, None, ALU.logical_shift_right))
            chain(nc.vector.tensor_copy(ntile[:], cnti[:]))
            chain(nc.vector.tensor_tensor_scan(cum[:], ones_e[:], ntile[:], 0.0, ALU.mult,
                                               ALU.add))
            chain(nc.vector.tensor_tensor(first[:], cum[:], ntile[:], ALU.subtract))
            chain(nc.vector.scalar_tensor_tensor(first[:], first[:], -float(TILE),
                                                 keep["ebase"][0:1, :], ALU.mult, ALU.add))
            wide = [1, NT, NE]
            t_w = ti[:].rearrange("p (t o) -> p t o", o=1).to_broadcast(wide)
            chain(nc.vector.tensor_tensor(
                cmp[:], t_w, cum[:].rearrange("p (o e) -> p o e", o=1).to_broadcast(wide),
                ALU.is_ge))
            chain(nc.vector.tensor_reduce(ef[:], cmp[:], AX.X, ALU.add))
            chain(nc.vector.tensor_scalar(valid[:], ef[:], float(NE), None, ALU.is_lt))
            chain(nc.vector.tensor_tensor(
                cmp[:], ef[:].rearrange("p (t o) -> p t o", o=1).to_broadcast(wide),
                keep["iota_e"][0:1, :].rearrange("p (o e) -> p o e", o=1).to_broadcast(wide),
                ALU.is_equal))
            chain(nc.vector.tensor_tensor(
                cmp[:], cmp[:], first[:].rearrange("p (o e) -> p o e", o=1).to_broadcast(wide),
                ALU.mult))
            chain(nc.vector.tensor_reduce(rowf[:], cmp[:], AX.X, ALU.add))
            chain(nc.vector.tensor_scalar(ti[:], ti[:], float(TILE), -float(NE * REGION),
                                          ALU.mult, ALU.add))
            chain(nc.vector.tensor_tensor(ti[:], ti[:], valid[:], ALU.mult))
            chain(nc.vector.scalar_tensor_tensor(rowf[:], rowf[:], float(NE * REGION), ti[:],
                                                 ALU.add, ALU.add))
            chain(nc.vector.tensor_scalar(tab_e[:], ef[:], float(NE - 1), None, ALU.min))
            nc.vector.tensor_copy(tab_r[:], rowf[:]).then_inc(table_ready, 1)

            dve.wait_ge(bdh_ready, 1)
            nc.vector.tensor_tensor(bdr[:], bdf[:], bds[:], ALU.subtract).then_inc(bd_link, 1)
            dve.wait_ge(bd_link, 1)
            nc.vector.tensor_copy(bds[32:64, :], bdr[32:64, :]).then_inc(bd_link, 1)
            nc.vector.tensor_copy(bdm[64:96, :], bdr[64:96, :]).then_inc(bd_link, 1)
            dve.wait_ge(bd_link, 3)
            nc.vector.tensor_tensor(bds[64:96, :], bdr[64:96, :], bdm[64:96, :], ALU.subtract
                                    ).then_inc(bd_ready, 1)

            def gate(t, q):
                e = dve.value_load(tab_e[0:1, bass.ds(t, 1)], min_val=0, max_val=NE - 1)
                dve.wait_ge(g_ps, t + 1)
                if not early(t, 2):
                    dve.wait_ge(sg_ready, t - 1)
                    dve.wait_ge(it_ready, t - 1)
                dve.sem_inc(e_passed, 1)
                for h in range(FH):
                    last = nc.vector.tensor_scalar(
                        gt[:, q, h * TILE:(h + 1) * TILE], pG[q][:, h * TILE:(h + 1) * TILE],
                        keep["bg"][:, bass.ds(e * FH + h, 1)], GATE_MAX, ALU.add, ALU.min)
                last.then_inc(g_ready, 1)
                return e

            def up(t, q, e):
                dve.wait_ge(u_ps, t + 1)
                dve.sem_inc(e_passed, 1)
                for h in range(FH):
                    last = nc.vector.tensor_scalar(
                        ut[:, q, h * TILE:(h + 1) * TILE], pU[q][:, h * TILE:(h + 1) * TILE],
                        keep["bu"][:, bass.ds(e * FH + h, 1)], GATE_MAX + 1.0, ALU.add, ALU.min)
                last.then_inc(u_ready, 1)

            def inner(t, q):
                dve.wait_ge(sg_ready, t + 1)
                nc.vector.tensor_tensor(gt[:, q], gt[:, q], sg[:, q], ALU.mult
                                        ).then_inc(glu_ready, 1)
                dve.wait_ge(glu_ready, t + 1)
                dve.wait_ge(u_ready, t + 1)
                if not early(t, 2):
                    dve.wait_ge(o_ps, t - 1)
                nc.vector.scalar_tensor_tensor(it[:, q], ut[:, q], 1.0 - GATE_MAX, gt[:, q],
                                               ALU.max, ALU.mult).then_inc(it_ready, 1)

            def tile(t, u):
                q = u % 2
                e = gate(t, q)
                if not early(t, 1):
                    inner(t - 1, 1 - q)
                up(t, q, e)

            schedule(dve, tile)
            inner(NT - 1, 1)

        @block.tensor
        def _(pe):
            mm = nc.tensor.matmul

            def turn(t, u):
                turns = 16 * (t // RING + 1) if isinstance(t, int) else (t - u) * (
                    16 // RING) + 16
                pe.wait_ge(rows_in[u], turns)
                if not early(t, 2):
                    pe.wait_ge(xT_ready, t - 1)
                for part in range(3):
                    for sx in range(2):
                        at = (part * 2 + sx) * P
                        last = nc.tensor.transpose(pX[u % 2][:, at:at + P],
                                                   xr[:, u, sx, part * DM:(part + 1) * DM],
                                                   identb[:])
                last.then_inc(xT_ps, 1)

            def gate_up(t, u):
                q = u % 2
                e = pe.value_load(tab_e[0:1, bass.ds(t, 1)], min_val=0, max_val=NE - 1)
                pe.wait_ge(xT_ready, t + 1)
                for m, (ps, done, left) in enumerate(((pG, g_ps, g_ready), (pU, u_ps, u_ready))):
                    if not early(t, 2):
                        pe.wait_ge(left, t - 1)
                    pe.sem_inc(e_passed, 1)
                    for h in range(FH):
                        for part in range(3):
                            last = mm(ps[q][:, h * TILE:(h + 1) * TILE],
                                      w_all[:, bass.ds(m * 4 * CW + (e * FH + h) * P, P)],
                                      xT[:, u % 4, part * TILE:(part + 1) * TILE],
                                      start=(part == 0), stop=(part == 2))
                    last.then_inc(done, 1)

            def down(t, q):
                e = pe.value_load(tab_e[0:1, bass.ds(t, 1)], min_val=0, max_val=NE - 1)
                pe.wait_ge(it_ready, t + 1)
                if not early(t, 2):
                    pe.wait_ge(y_ready, t - 1)
                pe.sem_inc(e_passed, 1)
                for sx in range(2):
                    dst = pO[q][:, sx * DM:(sx + 1) * DM]
                    mm(dst, pick[:], bds[:, bass.ds(e * DM, DM)], start=True, stop=False)
                    for h in range(FH):
                        last = mm(dst, it[:, q, h * TILE + sx * P:h * TILE + (sx + 1) * P],
                                  wd32[:, bass.ds((e * FH + h) * DM, DM)], start=False,
                                  stop=(h == FH - 1))
                last.then_inc(o_ps, 1)

            def tile(t, u):
                gate_up(t, u)
                if not early(t, LAG):
                    down(t - LAG, u % 2)
                if not late(t, LEAD):
                    turn(t + LEAD, (u + LEAD) % RING)

            pe.wait_ge(table_ready, 2)
            for t in range(LEAD):
                turn(t, t)
            pe.wait_ge(wd_ready, 1)
            pe.wait_ge(bd_ready, 1)
            pe.wait_ge(pick_made, 4)
            schedule(pe, tile)
            for t in range(NT - LAG, NT):
                down(t, t % 2)


def combine_phase(nc, keep, yk_d, x1_d, out):
    with ExitStack() as ctx:
        def sb(name, shape, dt=F32):
            return ctx.enter_context(nc.sbuf_tensor(name, shape, dt))

        def sem(name):
            return ctx.enter_context(nc.semaphore(name))

        SETS = 4
        yk = sb("yk", [P, SETS, JT, TOPK, DM])
        xm = sb("xm", [P, SETS, JT, DM])
        pair = sb("pair", [P, 2, JT, 2, DM])
        mo = sb("mo", [P, 2, JT, DM])
        res = sb("res", [P, 2, JT, DM])
        st = sb("stc", [P, 2, JT, 6])
        mv = sb("mvc", [P, 2, JT, 2])
        lnv, rr = sb("lnvc", [P, 2, JT]), sb("rrc", [P, 2, JT])
        eps = sb("epsc", [P, 1])
        yk_in = [sem(f"yk_in{q}") for q in range(SETS)]
        xm_in = [sem(f"xm_in{q}") for q in range(SETS)]
        stored = [sem(f"cstored{q}") for q in range(2)]
        eps_made, pair_ready, mo_ready, st_ready, v_ready, l_ready, r_ready, n_ready = (
            sem(n) for n in ("eps_made", "pair_ready", "mo_ready", "st_ready", "cv_ready",
                             "cl_ready", "cr_ready", "cn_ready"))
        res_ready, passed2 = sem("res_ready"), sem("passed2")
        block = ctx.enter_context(nc.Block())

        def schedule(eng, step):
            for c in range(SETS):
                step(c, c)
            with eng.Fori(1, NB // SETS) as i:
                for u in range(SETS):
                    step(i * SETS + u, u)

        def early(c, k):
            return isinstance(c, int) and c < k

        def arrived(c, u):
            return (16 * (c // SETS + 1) if isinstance(c, int)
                    else (c - u) * (16 // SETS) + 16)

        @block.sync
        def _(sp):
            def step(c, u):
                if not early(c, SETS):
                    sp.wait_ge(pair_ready, c - SETS + 1)
                sp.dma_start(yk[:, u].rearrange("p j k c -> p j (k c)"),
                             yk_d[bass.ds(c * L * TOPK, L * TOPK), :].rearrange(
                                 "(j p k) c -> p j (k c)", p=P, k=TOPK)).then_inc(yk_in[u], 16)
                if not early(c, SETS):
                    sp.wait_ge(res_ready, c - SETS + 1)
                sp.dma_start(xm[:, u], x1_d[bass.ds(c, 1)].rearrange(
                    "a (j p) c -> p (a j) c", p=P)).then_inc(xm_in[u], 16)

            schedule(sp, step)

        @block.gpsimd
        def _(pool):
            nc.gpsimd.memset(eps[:], EPS).then_inc(eps_made, 1)

            def step(c, u):
                pool.wait_ge(yk_in[u], arrived(c, u))
                if not early(c, 2):
                    pool.wait_ge(mo_ready, c - 1)
                pool.sem_inc(passed2, 1)
                nc.gpsimd.tensor_tensor(pair[:, u % 2], yk[:, u, :, 0:2], yk[:, u, :, 2:4],
                                        ALU.add).then_inc(pair_ready, 1)

            schedule(pool, step)

        @block.scalar
        def _(act):
            def step(c, u):
                q = u % 2
                act.wait_ge(v_ready, c + 1)
                nc.scalar.activation(lnv[:, q], mv[:, q, :, 1], ACT.Ln, bias=eps[:]
                                     ).then_inc(l_ready, 1)
                act.wait_ge(l_ready, c + 1)
                nc.scalar.activation(rr[:, q], lnv[:, q], ACT.Exp, scale=-0.5
                                     ).then_inc(r_ready, 1)
                act.wait_ge(res_ready, c + 1)
                act.dma_start(out[bass.ds(c, 1)].rearrange("a (j p) c -> p (a j) c", p=P),
                              res[:, q]).then_inc(stored[q], 16)

            nc.scalar.preload_act_table_set("natural_log_exp_and_others")
            act.wait_ge(eps_made, 1)
            schedule(act, step)
            for q in range(2):
                act.wait_ge(stored[q], NB * 8)

        @block.vector
        def _(dve):
            def total(c, u):
                q = u % 2
                dve.wait_ge(pair_ready, c + 1)
                if not early(c, 2):
                    dve.wait_ge(res_ready, c - 1)
                nc.vector.tensor_tensor(mo[:, q], pair[:, q, :, 0], pair[:, q, :, 1], ALU.add
                                        ).then_inc(mo_ready, 1)
                dve.wait_ge(mo_ready, c + 1)
                for j in range(JT):
                    last = nc.vector.bn_stats(st[:, q, j, :], mo[:, q, j])
                last.then_inc(st_ready, 1)
                dve.wait_ge(st_ready, c + 1)
                dve.sem_inc(passed2, 1)
                for j in range(JT):
                    last = nc.vector.bn_aggr(mv[:, q, j, :], st[:, q, j, :])
                last.then_inc(v_ready, 1)

            def finish(c, u):
                q = u % 2
                dve.wait_ge(r_ready, c + 1)
                for j in range(JT):
                    last = nc.vector.tensor_scalar(mo[:, q, j], mo[:, q, j], mv[:, q, j, 0:1],
                                                   rr[:, q, j:j + 1], ALU.subtract, ALU.mult)
                last.then_inc(n_ready, 1)
                dve.wait_ge(n_ready, c + 1)
                dve.wait_ge(xm_in[u], arrived(c, u))
                if not early(c, 2):
                    dve.wait_ge(stored[q], 16 * (c // 2) if isinstance(c, int) else (c - q) * 8)
                nc.vector.tensor_tensor(res[:, q], mo[:, q], xm[:, u], ALU.add
                                        ).then_inc(res_ready, 1)

            def step(c, u):
                total(c, u)
                if not early(c, 1):
                    finish(c - 1, (u - 1) % SETS)

            schedule(dve, step)
            finish(NB - 1, SETS - 1)


_INS = ['L0_attn_x', 'L0_attn_norm_w', 'L0_attn_norm_b', 'L0_attn_in_proj_w', 'L0_attn_conv_w',
        'L0_attn_conv_b', 'L0_attn_x_proj_w', 'L0_attn_dt_proj_w', 'L0_attn_dt_proj_b',
        'L0_attn_A_log', 'L0_attn_D_param', 'L0_attn_out_proj_w', 'L0_ffn_router_weight',
        'L0_ffn_router_bias', 'L0_ffn_gate_proj_bias', 'L0_ffn_up_proj_bias',
        'L0_ffn_down_proj_bias', 'L0_ffn_gate_proj_blocks', 'L0_ffn_gate_proj_scales',
        'L0_ffn_up_proj_blocks', 'L0_ffn_up_proj_scales', 'L0_ffn_down_proj_blocks',
        'L0_ffn_down_proj_scales']
_OUTS = [((NB, L, DM), 'float32')]


def kernel(**inputs):
    import numpy as _np
    import concourse.bacc as _bacc
    from concourse import mybir as _mybir
    from concourse.bass_utils import run_bass_kernel_spmd as _run

    nc = _bacc.Bacc("TRN2", target_bir_lowering=False, num_devices=1)
    arrays, args = {}, []
    for name in _INS:
        a = _np.ascontiguousarray(inputs[name])
        if a.dtype == _np.uint8:
            a = a.view(_np.uint32)
        arrays[f"in_{name}_dram"] = a
        args.append(nc.dram_tensor(f"in_{name}_dram", a.shape, _mybir.dt.from_np(a.dtype),
                                   kind="ExternalInput").ap())
    for i, (shape, dtype) in enumerate(_OUTS):
        dt = _mybir.dt.from_np(_np.dtype(dtype))
        args.append(nc.dram_tensor(f"out_{i}_dram", shape, dt, kind="ExternalOutput").ap())
    build(nc, *args)
    r = _run(nc, [arrays], core_ids=[0])
    return r.results[0]["out_0_dram"]
```
